# Optimizing a Trainium2 kernel written in Bass

```python
import numpy as np
import jax
import jax.numpy as jnp

def _softmax(x, axis=-1):
    return jax.nn.softmax(x, axis=axis)

def _gelu(x):
    return jax.nn.gelu(x, approximate=True)

def _silu(x):
    return jax.nn.silu(x)

def _sigmoid(x):
    return jax.nn.sigmoid(x)

def _layernorm(x, axis=-1, eps=1e-05):
    m = jnp.mean(x, axis=axis, keepdims=True)
    v = jnp.var(x, axis=axis, keepdims=True)
    return (x - m) / jnp.sqrt(v + eps)

def _scatter_add(tgt, idx, src, axis=0):
    return tgt.at[idx].add(src)

def _segment_sum(src, seg, n):
    return jax.ops.segment_sum(src, seg, n)
kernel_name = 'mk_sandwich_d2_jaxref_r4_734202'

def setup_inputs(seed: int=0):
    np.random.seed(seed)
    _w = jnp.asarray

    def _L0_attn_setup():
        import jax, jax.numpy as jnp
        import numpy as np
        B, N, D_IN, D_OUT = (8, 512, 256, 256)
        key = jax.random.key(seed)
        kx, kq, kk, kv = jax.random.split(key, 4)
        scale = 1.0 / np.sqrt(D_IN)
        return {'x': jax.random.normal(kx, (B, N, D_IN), dtype=jnp.float32), 'Wq': jax.random.normal(kq, (D_IN, D_OUT), dtype=jnp.float32) * scale, 'Wk': jax.random.normal(kk, (D_IN, D_OUT), dtype=jnp.float32) * scale, 'Wv': jax.random.normal(kv, (D_IN, D_OUT), dtype=jnp.float32) * scale}
    _L0_attn_in = _L0_attn_setup()

    def _L0_ffn_setup():
        import jax, jax.numpy as jnp
        import numpy as np
        INPUT_SIZE = 256
        OUTPUT_SIZE = 256
        key = jax.random.key(seed)
        kx, kt, kp, ktn, kpn = jax.random.split(key, 5)
        x = jax.random.normal(kx, (8, 512, INPUT_SIZE), dtype=jnp.float32)
        theta = jax.random.normal(kt, (INPUT_SIZE, OUTPUT_SIZE), dtype=jnp.float32) * 0.02
        phi = jax.random.normal(kp, (INPUT_SIZE, OUTPUT_SIZE), dtype=jnp.float32) * 0.02
        theta_noise = jax.random.normal(ktn, (INPUT_SIZE, OUTPUT_SIZE), dtype=jnp.float32) * 0.01
        phi_noise = jax.random.normal(kpn, (INPUT_SIZE, OUTPUT_SIZE), dtype=jnp.float32) * 0.01
        return {'x': x, 'theta': theta, 'phi': phi, 'theta_noise': theta_noise, 'phi_noise': phi_noise}
    _L0_ffn_in = _L0_ffn_setup()

    def _L1_attn_setup():
        import jax, jax.numpy as jnp
        import numpy as np
        B, S, D, H = (4, 512, 256, 16)
        DK = D // H
        key = jax.random.key(seed)
        k1, k2, k3 = jax.random.split(key, 3)
        x = jax.random.normal(k1, (B, S, D), dtype=jnp.float32)
        bound = 1.0 / np.sqrt(D)
        w_qkv = jax.random.uniform(k2, (3, H, DK, D), dtype=jnp.float32, minval=-bound, maxval=bound)
        w_o = jax.random.uniform(k3, (D, D), dtype=jnp.float32, minval=-bound, maxval=bound)
        return {'x': x, 'w_qkv': w_qkv, 'w_o': w_o}
    _L1_attn_in = _L1_attn_setup()

    def _L1_ffn_setup():
        import jax, jax.numpy as jnp
        import numpy as np
        D_IN, D_HID = (256, 1024)

        def _ternary(key, shape):
            return jax.random.randint(key, shape, -1, 2).astype(jnp.float32)

        def _tlin(x, w, s):
            return jnp.einsum('bsi,oi->bso', x, w) * s
        key = jax.random.key(seed)
        ks = jax.random.split(key, 12)
        inv = lambda fan: 1.0 / np.sqrt(fan).astype(np.float32)
        return {'x': jax.random.normal(ks[0], (4, 512, D_IN), dtype=jnp.float32), 'w1_w': _ternary(ks[1], (D_HID, D_IN)), 'w1_s': jax.random.uniform(ks[2], (D_HID,), dtype=jnp.float32) * inv(D_IN), 'w2_w': _ternary(ks[3], (D_HID, D_IN)), 'w2_s': jax.random.uniform(ks[4], (D_HID,), dtype=jnp.float32) * inv(D_IN), 'h1_w': _ternary(ks[5], (D_HID, D_HID)), 'h1_s': jax.random.uniform(ks[6], (D_HID,), dtype=jnp.float32) * inv(D_HID), 'h2_w': _ternary(ks[7], (D_HID, D_HID)), 'h2_s': jax.random.uniform(ks[8], (D_HID,), dtype=jnp.float32) * inv(D_HID), 'w3_w': _ternary(ks[9], (D_IN, D_HID)), 'w3_s': jax.random.uniform(ks[10], (D_IN,), dtype=jnp.float32) * inv(D_HID)}
    _L1_ffn_in = _L1_ffn_setup()
    _d = {'L0_attn_x': _L0_attn_in['x'], 'L0_attn_Wq': _L0_attn_in['Wq'], 'L0_attn_Wk': _L0_attn_in['Wk'], 'L0_attn_Wv': _L0_attn_in['Wv'], 'L0_ffn_theta': _L0_ffn_in['theta'], 'L0_ffn_phi': _L0_ffn_in['phi'], 'L0_ffn_theta_noise': _L0_ffn_in['theta_noise'], 'L0_ffn_phi_noise': _L0_ffn_in['phi_noise'], 'L1_attn_w_qkv': _L1_attn_in['w_qkv'], 'L1_attn_w_o': _L1_attn_in['w_o'], 'L1_ffn_w1_w': _L1_ffn_in['w1_w'], 'L1_ffn_w1_s': _L1_ffn_in['w1_s'], 'L1_ffn_w2_w': _L1_ffn_in['w2_w'], 'L1_ffn_w2_s': _L1_ffn_in['w2_s'], 'L1_ffn_h1_w': _L1_ffn_in['h1_w'], 'L1_ffn_h1_s': _L1_ffn_in['h1_s'], 'L1_ffn_h2_w': _L1_ffn_in['h2_w'], 'L1_ffn_h2_s': _L1_ffn_in['h2_s'], 'L1_ffn_w3_w': _L1_ffn_in['w3_w'], 'L1_ffn_w3_s': _L1_ffn_in['w3_s']}
    _x0 = _d['L0_attn_x']
    _d['L0_attn_x'] = jax.random.normal(jax.random.fold_in(jax.random.key(seed), 1), (4, 1024, 256), dtype=_x0.dtype)
    del _x0
    return _d

def reference(L0_attn_x, L0_attn_Wq, L0_attn_Wk, L0_attn_Wv, L0_ffn_theta, L0_ffn_phi, L0_ffn_theta_noise, L0_ffn_phi_noise, L1_attn_w_qkv, L1_attn_w_o, L1_ffn_w1_w, L1_ffn_w1_s, L1_ffn_w2_w, L1_ffn_w2_s, L1_ffn_h1_w, L1_ffn_h1_s, L1_ffn_h2_w, L1_ffn_h2_s, L1_ffn_w3_w, L1_ffn_w3_s):

    def _L0_attn_ref(x, Wq, Wk, Wv):
        import jax, jax.numpy as jnp
        import numpy as np
        B, N, D_IN, D_OUT = (8, 512, 256, 256)
        q = x @ Wq
        k = x @ Wk
        v = x @ Wv
        n = x.shape[1]
        scores = jnp.einsum('bqd,bkd->bqk', q, k)
        causal_mask = jnp.triu(jnp.ones((n, n), dtype=bool), k=1)
        scores = jnp.where(causal_mask, -jnp.inf, scores)
        inv_sqrt_d = jnp.asarray(1.0 / np.sqrt(q.shape[-1]), dtype=scores.dtype)
        attn = jax.nn.softmax(scores * inv_sqrt_d, axis=-1)
        return jnp.einsum('bqk,bkd->bqd', attn, v)

    def _L0_ffn_ref(x, theta, phi, theta_noise, phi_noise):
        import jax, jax.numpy as jnp
        import numpy as np
        INPUT_SIZE = 256
        OUTPUT_SIZE = 256
        real = jnp.einsum('bti,io->bto', x, jnp.cos(theta + theta_noise))
        imag = jnp.einsum('bti,io->bto', x, jnp.sin(phi + phi_noise))
        return jnp.sqrt(real * real + imag * imag)

    def _L1_attn_ref(x, w_qkv, w_o):
        import jax, jax.numpy as jnp
        import numpy as np
        B, S, D, H = (4, 512, 256, 16)
        DK = D // H
        seq_len = x.shape[-2]
        d_k = w_qkv.shape[-2]
        qkv = jnp.einsum('bsm,qhkm->qbhsk', x, w_qkv)
        Q, K, V = (qkv[0], qkv[1], qkv[2])
        scores = jnp.einsum('bhqk,bhsk->bhqs', Q, K) / jnp.sqrt(jnp.float32(d_k))
        causal = jnp.triu(jnp.ones((seq_len, seq_len), dtype=bool), k=1)
        scores = jnp.where(causal, -jnp.inf, scores)
        probs = jax.nn.softmax(scores, axis=-1)
        attn = jnp.einsum('bhqs,bhsk->bhqk', probs, V)
        attn = jnp.transpose(attn, (0, 2, 1, 3)).reshape(x.shape[0], seq_len, -1)
        return jnp.einsum('bsd,md->bsm', attn, w_o)

    def _L1_ffn_ref(x, w1_w, w1_s, w2_w, w2_s, h1_w, h1_s, h2_w, h2_s, w3_w, w3_s):
        import jax, jax.numpy as jnp
        import numpy as np
        D_IN, D_HID = (256, 1024)

        def _ternary(key, shape):
            return jax.random.randint(key, shape, -1, 2).astype(jnp.float32)

        def _tlin(x, w, s):
            return jnp.einsum('bsi,oi->bso', x, w) * s
        h = jax.nn.silu(_tlin(x, w1_w, w1_s)) * _tlin(x, w2_w, w2_s)
        h = jax.nn.gelu(_tlin(h, h1_w, h1_s), approximate=False)
        h = jax.nn.gelu(_tlin(h, h2_w, h2_s), approximate=False)
        return _tlin(h, w3_w, w3_s)
    x = L0_attn_x
    x = x + _layernorm(_L0_attn_ref(_layernorm(x, axis=-1), L0_attn_Wq, L0_attn_Wk, L0_attn_Wv), axis=-1)
    x = x + _layernorm(_L0_ffn_ref(_layernorm(x, axis=-1), L0_ffn_theta, L0_ffn_phi, L0_ffn_theta_noise, L0_ffn_phi_noise), axis=-1)
    x = x + _layernorm(_L1_attn_ref(_layernorm(x, axis=-1), L1_attn_w_qkv, L1_attn_w_o), axis=-1)
    x = x + _layernorm(_L1_ffn_ref(_layernorm(x, axis=-1), L1_ffn_w1_w, L1_ffn_w1_s, L1_ffn_w2_w, L1_ffn_w2_s, L1_ffn_h1_w, L1_ffn_h1_s, L1_ffn_h2_w, L1_ffn_h2_s, L1_ffn_w3_w, L1_ffn_w3_s), axis=-1)
    return x

_drawn_inputs = setup_inputs


def setup_inputs(seed=0):
    import zlib

    import numpy as np

    out = dict(_drawn_inputs(seed))
    spreads = {}
    factors = {'L0_ffn_theta': 8.0, 'L0_ffn_theta_noise': 8.0}
    for name, (base, spread) in spreads.items():
        noise = np.random.default_rng([zlib.crc32(name.encode()), seed]).standard_normal(out[name].shape)
        drawn = base * np.exp(spread * noise) if base else spread * noise
        out[name] = jnp.asarray(drawn.astype(out[name].dtype))
    for name, factor in factors.items():
        out[name] = (out[name] * factor).astype(out[name].dtype)
    return out
```

```python
from contextlib import ExitStack

import concourse.bass as bass
import numpy as np
from concourse import mybir

B, S, D = 4, 1024, 256
HID = 1024
H, DK = 16, 16
P = 128
BANK = 512
KC = D // P
HC = HID // P
ST = S // P
HALF = 4
NT = B * ST
EPS = 1e-5
NEG = -3.0e38

f32 = mybir.dt.float32
f32r = mybir.dt.float32r
bf16 = mybir.dt.bfloat16
ALU = mybir.AluOpType
ACT = mybir.ActivationFunctionType
AX = mybir.AxisListType


class Signal:

    def __init__(self, sem):
        self.sem, self.value = sem, 0


class Engine:

    def __init__(self):
        self.queue, self.waited = [], {}

    def wait(self, *marks):
        for mark in marks:
            if mark is None:
                continue
            signal, value = mark
            if self.waited.get(signal, 0) < value:
                self.waited[signal] = value
                self.queue.append(lambda e, s=signal.sem, v=value: e.wait_ge(s, v))

    def do(self, op, signal=None, by=1):
        if signal is None:
            self.queue.append(op)
            return None
        signal.value += by
        self.queue.append(lambda e: op(e).then_inc(signal.sem, by))
        return signal, signal.value

    def dma(self, out, in_, signal):
        out, in_ = (ap.bitcast(f32) if ap.dtype == f32r else ap for ap in (out, in_))
        return self.do(lambda e: e.dma_start(out, in_), signal, 16)

    def emit(self, e):
        for op in self.queue:
            op(e)


def sandwich(nc, x_in, wq0, wk0, wv0, theta, phi, theta_n, phi_n, wqkvT, woT, w1T, w2T, h1T, h2T,
             w3T, s1, s2, sh1, sh2, s3, out):
    pe, act, dve, pool, sp = (Engine() for _ in range(5))
    engines = (pe, act, dve, pool, sp)
    ctx = ExitStack()
    with ctx:
        signals = []

        def signal(name):
            signals.append(Signal(ctx.enter_context(nc.semaphore(name))))
            return signals[-1]

        def sb(where, name, shape, dt=f32):
            return where.enter_context(nc.sbuf_tensor(name, shape, dt))

        psum = ctx.enter_context(nc.psum_tensor("psum", [P, 8, BANK], f32))
        bank_free = [[] for _ in range(8)]

        def mm(o, l, r, start, stop, done=None):
            return pe.do(lambda e: e.matmul(o, l, r, start=start, stop=stop), done)

        def plain(ap):
            return ap.bitcast(f32)

        ld = [signal(f"ld{i}") for i in range(6)]
        ld_x = [signal(f"ld_x{b}") for b in range(B)]
        pool_const = signal("pool_const")
        dve_stat = signal("dve_stat")
        act_std = signal("act_std")
        dve_norm = signal("dve_norm")
        pool_res = signal("pool_res")
        pe_tr = signal("pe_tr")
        act_hi = signal("act_hi")
        dve_lo = signal("dve_lo")
        pe_prod = signal("pe_prod")
        act_out = signal("act_out")
        dve_out = signal("dve_out")
        pe_s = signal("pe_s")
        pe_pv = signal("pe_pv")
        dve_max = signal("dve_max")
        act_exp = signal("act_exp")
        pool_mask = signal("pool_mask")
        pe_max = signal("pe_max")
        dve_m = signal("dve_m")
        act_m = signal("act_m")
        pe_m = signal("pe_m")
        dma_m = [signal(f"dma_m{i}") for i in range(3)]
        dma_stack = [signal(f"dma_stack{i}") for i in range(3)]
        dve_w = signal("dve_w")
        act_w = signal("act_w")
        pe_h = signal("pe_h")
        act_h = signal("act_h")
        dve_h = signal("dve_h")
        st_out = signal("st_out")

        def barrier():
            for e in engines:
                e.wait(*[(s, s.value) for s in signals if s.value])
            for marks in bank_free:
                marks.clear()

        ident = sb(ctx, "ident", [P, P])
        ident16 = sb(ctx, "ident16", [P, P], bf16)
        tri16 = sb(ctx, "tri16", [P, P], bf16)
        eps = sb(ctx, "eps", [P, 1])
        x = sb(ctx, "x", [P, NT, D])
        room = {}
        stat = sb(ctx, "stat", [P, HALF, 6])
        mv = sb(ctx, "mv", [P, HALF, 2])
        std = sb(ctx, "std", [P, HALF])
        rstd = sb(ctx, "rstd", [P, HALF])

        for b in range(B):
            x_mark = sp.dma(x[:, b * ST:(b + 1) * ST, :], x_in[b].rearrange("(t p) d -> p t d", p=P), ld_x[b])
        x_ready = [[(ld_x[b], 16)] * ST for b in range(B)]
        x_ready = [m for marks in x_ready for m in marks]

        c = [pool.do(lambda e: e.memset(ident[:, :], 0.0), pool_const),
             pool.do(lambda e: e.memset(ident16[:, :], 0.0), pool_const),
             pool.do(lambda e: e.memset(tri16[:, :], 0.0), pool_const),
             pool.do(lambda e: e.memset(eps[:, :], EPS), pool_const)]
        pool.wait(c[-1])
        for t in (ident, ident16):
            pool.do(lambda e, t=t: e.affine_select(out=t[:, :], in_=t[:, :], compare_op=ALU.not_equal, fill=1.0,
                                                   base=0, pattern=[[-1, P]], channel_multiplier=1), pool_const)
        const_ready = pool.do(lambda e: e.affine_select(out=tri16[:, :], in_=tri16[:, :], compare_op=ALU.is_ge,
                                                        fill=NEG, base=0, pattern=[[-1, P]],
                                                        channel_multiplier=1), pool_const)
        act.wait(const_ready)
        pe.wait(const_ready)

        free = {"xn": [[], []], "y": [[], []]}

        def normalise(src, ready, put):
            dve.wait(*ready)
            for t in range(HALF):
                m = dve.do(lambda e, t=t: e.bn_stats(stat[:, t, :], src(t)), dve_stat)
            for t in range(HALF):
                dve.wait((dve_stat, m[1] - HALF + 1 + t))
                v = dve.do(lambda e, t=t: e.bn_aggr(mv[:, t, :], stat[:, t, :]), dve_stat)
            act.wait(v)
            s = act.do(lambda e: e.activation(std[:, :], mv[:, :, 1], ACT.Sqrt, bias=eps[:, :]), act_std)
            dve.wait(s)
            r = dve.do(lambda e: e.reciprocal(rstd[:, :], std[:, :]), dve_stat)
            dve.wait(r)
            return [put(t, mv[:, t, 0:1], rstd[:, t:t + 1]) for t in range(HALF)]

        def room_for(where, layer, n_xn, y=None):
            room["xn"] = sb(where, f"xn{layer}", [P, n_xn, HALF, D])
            room["y"] = sb(where, f"y{layer}", [P, 2, HALF, D]) if y is None else y
            free["xn"], free["y"] = [[] for _ in range(n_xn)], [[], []]

        def norm_in(b, half):
            xn = room["xn"]
            k, t0 = half % len(free["xn"]), b * ST + half * HALF
            dve.wait(*free["xn"][k])
            free["xn"][k] = []
            return normalise(
                lambda t: x[:, t0 + t, :], x_ready[t0:t0 + HALF],
                lambda t, m, r: dve.do(lambda e: e.tensor_scalar(xn[:, k, t, :], x[:, t0 + t, :], m, r,
                                                                 ALU.subtract, ALU.mult), dve_norm))

        def add_out(b, half, y_ready):
            y = room["y"]
            k, t0 = half, b * ST + half * HALF
            marks = normalise(
                lambda t: y[:, k, t, :], y_ready,
                lambda t, m, r: dve.do(lambda e: e.tensor_scalar(y[:, k, t, :], y[:, k, t, :], m, r,
                                                                 ALU.subtract, ALU.mult), dve_norm))
            pool.wait(marks[-1])
            done = pool.do(lambda e: e.tensor_tensor(x[:, t0:t0 + HALF, :], x[:, t0:t0 + HALF, :],
                                                     y[:, k, :, :], ALU.add), pool_res)
            free["y"][k] = [done]
            x_ready[t0:t0 + HALF] = [done] * HALF
            return done

        def evac_split(bank, src, hi, lo, before=()):
            act.wait(*before)
            h = act.do(lambda e: e.activation(hi, src, ACT.Copy), act_hi)
            dve.wait(*before)
            dve.wait(h)
            m = dve.do(lambda e: e.tensor_tensor(lo, src, plain(hi), ALU.subtract), dve_lo)
            bank_free[bank] = [m]
            return m

        def transpose_half(bank, src, ready, c, hi, lo, wait_free):
            pe.wait(*bank_free[bank], *ready)
            for t in range(HALF):
                m = pe.do(lambda e, t=t: e.transpose(psum[:, bank, t * P:(t + 1) * P],
                                                     src[:, t, c * P:(c + 1) * P], ident[:, :]),
                          pe_tr if t == HALF - 1 else None)
            act.wait(m)
            return m, evac_split(bank, psum[:, bank, :], hi, lo, wait_free)

        def mm_split(o, terms, done, start=True, stop=True):
            ops = [p for (lh, ll), (rh, rl) in terms for p in ((lh, rh), (lh, rl), (ll, rh))]
            for n, (l, r) in enumerate(ops):
                last = n == len(ops) - 1
                m = mm(o, l, r, start and n == 0, stop and last, done if last else None)
            return m

        def split_weight(where, name, src, shape, sig):
            hi, lo = sb(where, name + "_hi", shape, f32r), sb(where, name + "_lo", shape, f32r)
            with ExitStack() as tmp:
                raw = sb(tmp, name + "_raw", shape)
                m = sp.dma(raw[:, :, :], src, sig)
                act.wait(m)
                h = act.do(lambda e: e.activation(hi[:, :, :], raw[:, :, :], ACT.Copy), act_w)
                dve.wait(m, h)
                w = dve.do(lambda e: e.tensor_tensor(lo[:, :, :], raw[:, :, :], plain(hi[:, :, :]), ALU.subtract), dve_w)
            sp.wait(w)
            act.wait(w)
            return (hi, lo), w

        def rows(w):
            return w.rearrange("(c p) n -> p c n", p=P)

        def spread(units, steps):
            n = len(units)
            return [units[n * i // steps:n * (i + 1) // steps] for i in range(steps)]

        early = ctx.enter_context(ExitStack())
        trig = [sb(early, "trig_hi", [P, KC, 2 * D], f32r), sb(early, "trig_lo", [P, KC, 2 * D], f32r)]
        TWO_PI = 2 * np.pi
        C1 = 6.28125
        C2 = float(np.float32(TWO_PI - C1))
        C3 = float(TWO_PI - C1 - C2)
        PI_BELOW = float(np.nextafter(np.float32(np.pi), np.float32(0)))
        ROUND = 1.5 * 2.0 ** 23
        with ExitStack() as tmp:
            ang = sb(tmp, "ang", [P, 2, KC, D])
            noise = sb(tmp, "noise", [P, 2, KC, D])
            turns = sb(tmp, "turns", [P, 2, KC, D])
            wave = sb(tmp, "wave", [P, 2, KC, D])
            for n, (w, s) in enumerate(((theta, ang), (phi, ang), (theta_n, noise), (phi_n, noise))):
                a = sp.dma(s[:, n % 2, :, :], rows(w), ld[4])
            dve.wait(a)
            m = dve.do(lambda e: e.tensor_tensor(ang[:, :, :, :], ang[:, :, :, :], noise[:, :, :, :], ALU.add), dve_w)
            for n, turn in ((0, 0.25), (1, 0.0)):
                dve.wait(m)
                m = dve.do(lambda e, n=n, turn=turn: e.tensor_scalar(
                    turns[:, n, :, :], ang[:, n, :, :], 1 / TWO_PI, turn, ALU.mult, ALU.add), dve_w)
            for c in (ROUND, -ROUND):
                dve.wait(m)
                m = dve.do(lambda e, c=c: e.tensor_scalar(turns[:, :, :, :], turns[:, :, :, :], c, None, ALU.add), dve_w)
            for c in (C1, C2, C3):
                dve.wait(m)
                m = dve.do(lambda e, c=c: e.scalar_tensor_tensor(
                    ang[:, :, :, :].rearrange("p a c d -> p (a c d)"), turns[:, :, :, :].rearrange("p a c d -> p (a c d)"),
                    -c, ang[:, :, :, :].rearrange("p a c d -> p (a c d)"), ALU.mult, ALU.add), dve_w)
            dve.wait(m)
            m = dve.do(lambda e: e.tensor_scalar(ang[:, 0, :, :], ang[:, 0, :, :], float(np.pi / 2), None, ALU.add), dve_w)
            dve.wait(m)
            m = dve.do(lambda e: e.tensor_scalar(ang[:, :, :, :], ang[:, :, :, :], PI_BELOW, -PI_BELOW,
                                                 ALU.min, ALU.max), dve_w)
            act.wait(m)
            m = act.do(lambda e: e.activation(wave[:, :, :, :], ang[:, :, :, :], ACT.Sin), act_w)
            act.wait(m)
            for n in range(2):
                m = act.do(lambda e, n=n: e.activation(trig[0][:, :, n * D:(n + 1) * D], wave[:, n, :, :], ACT.Copy), act_w)
            dve.wait(m)
            for n in range(2):
                trig_ready = dve.do(lambda e, n=n: e.tensor_tensor(
                    trig[1][:, :, n * D:(n + 1) * D], wave[:, n, :, :], plain(trig[0][:, :, n * D:(n + 1) * D]),
                    ALU.subtract), dve_w)
        sp.wait(trig_ready)

        SC0 = 1.0 / D ** 0.5
        def layer1(ph):
            room_for(ph, 1, 2)
            xn, y = room["xn"], room["y"]
            wts = []
            for n, w in enumerate((wq0, wk0, wv0)):
                t, w_ready = split_weight(ph, f"w0{n}", rows(w), [P, KC, D], ld[n])
                wts.append(t)
            pe.wait(w_ready)
            xT = [sb(ph, f"xT0_{k}", [P, KC, S], f32r) for k in ("hi", "lo")]
            qT = [[sb(ph, f"qT{i}_{k}", [P, KC, S], f32r) for k in ("hi", "lo")] for i in range(2)]
            kT = [[sb(ph, f"kT{i}_{k}", [P, KC, S], f32r) for k in ("hi", "lo")] for i in range(2)]
            v = [[sb(ph, f"v{i}_{k}", [P, ST, D], f32r) for k in ("hi", "lo")] for i in range(2)]
            prob = sb(ph, "prob", [P, 2, S])
            pT = [sb(ph, f"pT_{k}", [P, ST, P], f32r) for k in ("hi", "lo")]
            mx = sb(ph, "mx0", [P, 2])
            nb = sb(ph, "nb0", [P, 2])
            den = sb(ph, "den0", [P, 2])
            rden = sb(ph, "rden0", [P, 2])
            xT_free, qkv_free = [], [[], []]
            SIDE, TB = 7, (4, 5)
            O = 6

            def pre_units(b):
                def norm(half):
                    norms[half] = norm_in(b, half)

                def tr(half, c):
                    cols = slice(half * BANK, (half + 1) * BANK)
                    m, done = transpose_half(SIDE, xn[:, half, :, :], norms[half], c, xT[0][:, c, cols], xT[1][:, c, cols],
                                             xT_free)
                    free["xn"][half] = [m]
                    xT_ready[(b, half)] = done
                norms = {}
                return [lambda: norm(0), lambda: tr(0, 0), lambda: tr(0, 1), lambda: norm(1), lambda: tr(1, 0), lambda: tr(1, 1)]

            def proj_units(b):
                def qk(dst, w, c, half):
                    pe.wait(*bank_free[SIDE], xT_ready[(b, half)])
                    cols = slice(half * BANK, (half + 1) * BANK)
                    m = mm_split(psum[:, SIDE, :], [((w[0][:, k, c * P:(c + 1) * P], w[1][:, k, c * P:(c + 1) * P]),
                                                     (xT[0][:, k, cols], xT[1][:, k, cols])) for k in range(KC)], pe_prod)
                    act.wait(m)
                    qkv_ready[b] = evac_split(SIDE, psum[:, SIDE, :], dst[0][:, c, cols], dst[1][:, c, cols], qkv_free[b % 2])
                    return m

                def val(t):
                    pe.wait(*bank_free[SIDE], xT_ready[(b, 1)])
                    w = wts[2]
                    for n in range(2):
                        tok = slice((t + n) * P, (t + n + 1) * P)
                        m = mm_split(psum[:, SIDE, n * D:(n + 1) * D], [((xT[0][:, k, tok], xT[1][:, k, tok]),
                                                                         (w[0][:, k, :], w[1][:, k, :])) for k in range(KC)],
                                     pe_prod)
                    act.wait(m)
                    qkv_ready[b] = evac_split(SIDE, psum[:, SIDE, :].rearrange("p (t d) -> p t d", t=2),
                                              v[b % 2][0][:, t:t + 2, :], v[b % 2][1][:, t:t + 2, :], qkv_free[b % 2])
                    xT_free[:] = [m]
                return ([lambda c=c, half=half, dst=dst, w=w: qk(dst, w, c, half)
                         for half in range(2) for dst, w in ((qT[b % 2], wts[0]), (kT[b % 2], wts[1])) for c in range(KC)]
                        + [lambda t=t: val(t) for t in range(0, ST, 2)])

            xT_ready, qkv_ready = {}, {}
            y_ready = {}
            st = {}

            def scores(b, i):
                n, Q, K = b * ST + i, qT[b % 2], kT[b % 2]
                k = n % 2
                pair = (2 * k, 2 * k + 1)
                pe.wait(*bank_free[pair[0]], qkv_ready[b])
                tok = slice(i * P, (i + 1) * P)
                w_all = (i + 1) * P
                for c0 in range(0, w_all, BANK):
                    w = min(BANK, w_all - c0)
                    mm_split(psum[:, pair[c0 // BANK], 0:w],
                             [((Q[0][:, kk, tok], Q[1][:, kk, tok]), (K[0][:, kk, c0:c0 + w], K[1][:, kk, c0:c0 + w]))
                              for kk in range(KC)], None, stop=c0 + w < w_all)
                d = i * P % BANK
                m = mm(psum[:, pair[i * P // BANK], d:d + P], ident16[:, :], tri16[:, :], False, True, pe_s)
                src = psum[:, pair[0]:pair[0] + 2, :].rearrange("p a n -> p (a n)")[:, 0:w_all]
                dve.wait(m, *st.get(("exp", n - 2), []))
                a = dve.do(lambda e: e.tensor_reduce(mx[:, k:k + 1], src, AX.X, ALU.max), dve_max)
                dve.wait(a)
                a = dve.do(lambda e: e.tensor_scalar(nb[:, k:k + 1], mx[:, k:k + 1], -SC0, None, ALU.mult), dve_max)
                act.wait(a, *st.get(("pT", n - 2), []), *st.get(("rden", n - 2), []))
                ex = act.do(lambda e: e.activation(prob[:, k, 0:w_all], src, ACT.Exp, bias=nb[:, k:k + 1], scale=SC0,
                                                   accum_out=den[:, k:k + 1]), act_exp)
                bank_free[pair[0]] = bank_free[pair[1]] = [ex]
                st[("exp", n)] = [ex]
                dve.wait(ex)
                rd = dve.do(lambda e: e.reciprocal(rden[:, k:k + 1], den[:, k:k + 1]), dve_max)
                st[("rden", n)] = [rd]

            def turn(b, i):
                n = b * ST + i
                k = n % 2
                pe.wait(*st[("exp", n)])
                for k0 in range(0, i + 1, 4):
                    kk = min(4, i + 1 - k0)
                    bank = TB[(k0 // 4) % 2]
                    pe.wait(*bank_free[bank])
                    for j in range(kk):
                        m = pe.do(lambda e, j=j, bank=bank, k0=k0: e.transpose(psum[:, bank, j * P:(j + 1) * P],
                                                                  prob[:, k, (k0 + j) * P:(k0 + j + 1) * P], ident[:, :]),
                                  pe_tr)
                    act.wait(m)
                    st[("pTr", n)] = [evac_split(bank, psum[:, bank, 0:kk * P].rearrange("p (k q) -> p k q", q=P),
                                                 pT[0][:, k0:k0 + kk, :], pT[1][:, k0:k0 + kk, :],
                                                 st.get(("pv", n - 1), []))]
                st[("pT", n)] = [m]

            def weigh(b, i):
                n, V = b * ST + i, v[b % 2]
                half, t = i // HALF, i % HALF
                pe.wait(*st[("pTr", n)], *bank_free[O])
                m = mm_split(psum[:, O, 0:D], [((pT[0][:, j, :], pT[1][:, j, :]), (V[0][:, j, :], V[1][:, j, :]))
                                               for j in range(i + 1)], pe_pv)
                st[("pv", n)] = [m]
                act.wait(m, *st[("rden", n)], *free["y"][half])
                o = act.do(lambda e: e.activation(y[:, half, t, :], psum[:, O, 0:D], ACT.Copy,
                                                  scale=rden[:, n % 2:n % 2 + 1]), act_out)
                st[("rden", n)] = [o]
                bank_free[O] = [o]
                if i == ST - 1:
                    qkv_free[b % 2] = [m]
                if t == HALF - 1:
                    add_out(b, half, [o])

            for u in pre_units(0) + proj_units(0):
                u()
            for b in range(B):
                side = spread(pre_units(b + 1) + proj_units(b + 1) if b + 1 < B else [], ST)
                for i in range(ST):
                    n = b * ST + i
                    scores(b, i)
                    if n >= 1:
                        turn(*divmod(n - 1, ST))
                    for u in side[i]:
                        u()
                    if n >= 1:
                        weigh(*divmod(n - 1, ST))
            turn(B - 1, ST - 1)
            weigh(B - 1, ST - 1)
            barrier()

        with ExitStack() as ph:
            layer1(ph)

        def layer2(ph):
            room_for(ph, 2, 2)
            xn, y = room["xn"], room["y"]
            xT = [[sb(ph, f"xT1_{i}{k}", [P, KC, BANK], f32r) for k in ("hi", "lo")] for i in range(2)]
            sq = sb(ph, "sq", [P, 2, 2 * D])
            pw = sb(ph, "pw", [P, 2, HALF, D])
            xT_free = [[], []]
            tr_banks, o_banks = (0, 1, 2, 3), (4, 5, 6, 7)
            ready = {}

            def pre_half(n):
                b, half = divmod(n, 2)
                k = n % 2
                norms = norm_in(b, half)
                for c in range(KC):
                    m, done = transpose_half(tr_banks[(2 * n + c) % 4], xn[:, half, :, :], norms, c, xT[k][0][:, c, :],
                                             xT[k][1][:, c, :], xT_free[k])
                free["xn"][half] = [m]
                ready[n] = done

            sq_free, pw_free = [[], []], [[], []]
            pe.wait(trig_ready)
            pre_half(0)
            for n in range(2 * B):
                if n + 1 < 2 * B:
                    pre_half(n + 1)
                b, half = divmod(n, 2)
                k = n % 2
                for t in range(HALF):
                    bank = o_banks[t]
                    pe.wait(*bank_free[bank], ready[n])
                    tok = slice(t * P, (t + 1) * P)
                    m = mm_split(psum[:, bank, :], [((xT[k][0][:, c, tok], xT[k][1][:, c, tok]),
                                                     (trig[0][:, c, :], trig[1][:, c, :])) for c in range(KC)], pe_prod)
                    q = t % 2
                    act.wait(m, *sq_free[q])
                    s_ = act.do(lambda e, q=q, bank=bank: e.activation(sq[:, q, :], psum[:, bank, :], ACT.Square), act_h)
                    bank_free[bank] = [s_]
                    dve.wait(s_, *pw_free[k])
                    d_ = dve.do(lambda e, q=q, k=k, t=t: e.tensor_tensor(pw[:, k, t, :], sq[:, q, 0:D], sq[:, q, D:2 * D],
                                                                         ALU.add), dve_h)
                    sq_free[q] = [d_]
                xT_free[k] = [m]
                act.wait(d_, *free["y"][half])
                o = act.do(lambda e, k=k, half=half: e.activation(y[:, half, :, :], pw[:, k, :, :], ACT.Sqrt), act_out)
                pw_free[k] = [o]
                add_out(b, half, [o])
            barrier()

        with ExitStack() as ph:
            layer2(ph)
        early.close()

        G = 4
        SC1 = 1.0 / DK ** 0.5
        NST = 3
        STEPS = [(c, j) for c in range(S // BANK) for j in range(4 * (c + 1))]
        NS = len(STEPS)
        LEAD = NS + 3
        QR, KR = 3 * DK + 2, 3 * DK
        def layer3(ph):
            (wa_hi, wa_lo), m1 = split_weight(ph, "wqkv", rows(wqkvT), [P, KC, 3 * D], ld[0])
            (wo_hi, wo_lo), m2 = split_weight(ph, "wo", rows(woT), [P, KC, D], ld[1])
            xT = [sb(ph, f"xT2_{k}", [P, KC, S], f32r) for k in ("hi", "lo")]
            nat = {"q": [sb(ph, f"q_{k}", [P, 2, S], f32r) for k in ("hi", "lo")],
                   "k": [sb(ph, f"k_{k}", [P, 2, S], f32r) for k in ("hi", "lo")]}
            VW = DK + 1
            VB = 2 * DK
            va = [sb(ph, f"va{i}", [P, ST, H * VW + VB - VW]) for i in range(2)]
            Qs = [sb(ph, f"Qs{i}", [P, 2, S], f32r) for i in range(NST)]
            Ks = [sb(ph, f"Ks{i}", [P, 2, S], f32r) for i in range(NST)]
            pr = sb(ph, "pr", [P, 4, 2, BANK])
            maskw = sb(ph, "maskw", [P, BANK])
            mxs = sb(ph, "mxs", [P, 2, 2, 2, ST])
            mT = [sb(ph, f"mT_{k}", [2 * 2 * ST, P], f32r) for k in ("hi", "lo")]
            oT = sb(ph, "oT", [P, BANK])
            attn = sb(ph, "attn", [P, ST, D])
            room_for(ph, 3, 1, attn[:, :, :].rearrange("p (h t) d -> p h t d", h=2))
            xn, y = room["xn"], room["y"]
            aT = [sb(ph, f"aT_{k}", [P, KC, BANK], f32r) for k in ("hi", "lo")]
            rd4 = sb(ph, "rd4", [P, HALF * 4])

            m = pool.do(lambda e: e.memset(maskw[:, :], 0.0), pool_const)
            pool.wait(m)
            pool.do(lambda e: e.affine_select(out=maskw[:, BANK - P:], in_=maskw[:, BANK - P:], compare_op=ALU.is_ge,
                                              fill=NEG, base=0, pattern=[[-1, P]], channel_multiplier=1), pool_const)
            for i in range(2):
                pool.do(lambda e, i=i: e.memset(va[i][:, :, :], 1.0), pool_const)
            for i in range(NST):
                init_ready = pool.do(lambda e, i=i: e.memset(Ks[i][:, :, :].bitcast(f32), 1.0), pool_const)
            for e in (pe, dve, act, sp):
                e.wait(init_ready)
            pe.wait(m1, m2)

            MAXB, SIDE, STB, PVB = (0, 1), 2, (3, 5), 7
            xT_free, nat_free, va_free = [], [], [[], []]
            xT_ready, nat_ready, va_ready = {}, {}, {}
            stack_ready, stack_free = {}, {}
            m_ready, max_done = {}, {}
            st = {}

            def pre3(b):
                norms = {}

                def norm(half):
                    norms[half] = norm_in(b, half)

                def tr(half, c):
                    cols = slice(half * BANK, (half + 1) * BANK)
                    m, done = transpose_half(SIDE, xn[:, 0, :, :], norms[half], c, xT[0][:, c, cols], xT[1][:, c, cols],
                                             xT_free)
                    free["xn"][0] = [m]
                    xT_ready[(b, half)] = done
                return [lambda: norm(0), lambda: tr(0, 0), lambda: tr(0, 1), lambda: norm(1), lambda: tr(1, 0), lambda: tr(1, 1)]

            def proj3(b):
                def qk(name, c, half):
                    o = (0 if name == "q" else D) + c * P
                    cols = slice(half * BANK, (half + 1) * BANK)
                    pe.wait(*bank_free[SIDE], xT_ready[(b, half)])
                    m = mm_split(psum[:, SIDE, :], [((wa_hi[:, k, o:o + P], wa_lo[:, k, o:o + P]),
                                                     (xT[0][:, k, cols], xT[1][:, k, cols])) for k in range(KC)], pe_prod)
                    act.wait(m)
                    hi, lo = nat[name]
                    nat_ready[b] = evac_split(SIDE, psum[:, SIDE, :], hi[:, c, cols], lo[:, c, cols], nat_free)

                def val(t):
                    pe.wait(*bank_free[SIDE], xT_ready[(b, 1)])
                    for n in range(2):
                        tok = slice((t + n) * P, (t + n + 1) * P)
                        m = mm_split(psum[:, SIDE, n * D:(n + 1) * D],
                                     [((xT[0][:, k, tok], xT[1][:, k, tok]), (wa_hi[:, k, 2 * D:], wa_lo[:, k, 2 * D:]))
                                      for k in range(KC)], pe_prod)
                    act.wait(m, *va_free[b % 2])
                    for n in range(2):
                        dst = va[b % 2][:, t + n, 0:H * VW].rearrange("p (h w) -> p h w", w=VW)[:, :, 0:DK]
                        o = act.do(lambda e, n=n, dst=dst: e.activation(
                            dst, psum[:, SIDE, n * D:(n + 1) * D].rearrange("p (h w) -> p h w", w=DK), ACT.Copy), act_out)
                    bank_free[SIDE] = [o]
                    va_ready[b] = o
                    xT_free[:] = [m]
                return ([lambda name=name, c=c, half=half: qk(name, c, half)
                         for half in range(2) for name in "qk" for c in range(2)]
                        + [lambda t=t: val(t) for t in range(0, ST, 2)])

            def load_stack(g):
                b, gl = divmod(g, G)
                i = g % NST
                sp.wait(nat_ready[b], *stack_free.get(g - NST, []))
                for side in range(2):
                    r = 32 * gl + DK * side
                    for k, (q_, k_) in enumerate(((0, 0), (1, 0), (0, 1))):
                        d = 64 * side + DK * k
                        sp.dma(Qs[i][d:d + DK, :, :], nat["q"][q_][r:r + DK, :, :], dma_stack[i])
                        m = sp.dma(Ks[i][d:d + DK, :, :], nat["k"][k_][r:r + DK, :, :], dma_stack[i])
                stack_ready[g] = m
                if gl == G - 1:
                    nat_free[:] = [m]

            max_blocks = [(i, k0, min(BANK, (i + 1) * P - k0)) for i in range(ST) for k0 in range(0, (i + 1) * P, BANK)]
            count = {"max": 0}

            def max_block(g, n):
                i, k0, w = max_blocks[n]
                buf, mb = g % NST, g % 2
                pe.wait(stack_ready[g])
                diag = k0 + w == (i + 1) * P
                if n == 0:
                    dve.wait(*st.get(("mread", g - 2), []))
                for pair in range(2):
                    for side in range(2):
                        bank = MAXB[count["max"] % 2]
                        count["max"] += 1
                        pe.wait(*bank_free[bank])
                        r = slice(64 * side, 64 * side + KR)
                        m = mm(psum[:, bank, 0:w], Qs[buf][r, pair, i * P:(i + 1) * P], Ks[buf][r, pair, k0:k0 + w],
                               True, True, pe_max)
                        dst = mxs[:, mb, side, pair, i:i + 1]
                        dve.wait(m)
                        if not diag:
                            a = dve.do(lambda e, bank=bank, dst=dst: e.tensor_reduce(dst, psum[:, bank, 0:w], AX.X, ALU.max),
                                       dve_max)
                            st[("part", side, pair)] = a
                        else:
                            first = NEG
                            if k0:
                                dve.wait(st[("part", side, pair)])
                                first = dst
                            a = dve.do(lambda e, bank=bank, dst=dst, first=first: e.tensor_tensor_reduce(
                                out=psum[:, bank, 0:w], in0=psum[:, bank, 0:w], in1=maskw[:, BANK - w:], scale=1.0, scalar=first,
                                op0=ALU.add, op1=ALU.max, accum_out=dst), dve_max)
                        bank_free[bank] = [a]
                max_done[g] = m
                st[("mx", g)] = a

            def put_max(g):
                buf, mb = g % NST, g % 2
                n = 2 * 2 * ST
                pe.wait(*bank_free[SIDE], st[("mx", g)])
                m = pe.do(lambda e: e.transpose(psum[0:n, SIDE, 0:P], mxs[:, mb, :, :, :].rearrange("p s a t -> p (s a t)"),
                                                ident[:, :]), pe_m)
                st[("mread", g)] = [m]
                act.wait(m, *st.get("m_sent", []))
                dve.wait(*st.get("m_sent", []))
                h = act.do(lambda e: e.activation(mT[0][:, :], psum[0:n, SIDE, 0:P], ACT.Copy, scale=-1.0), act_m)
                dve.wait(h)
                l = dve.do(lambda e: e.scalar_tensor_tensor(mT[1][:, :], psum[0:n, SIDE, 0:P], -1.0, plain(mT[0][:, :]),
                                                            ALU.mult, ALU.subtract), dve_m)
                bank_free[SIDE] = [l]
                sp.wait(h, l)
                for side in range(2):
                    for k in range(2):
                        d = 64 * side + KR + k
                        a = sp.dma(Qs[buf][d:d + 1, :, :].rearrange("o a (t q) -> o (a t) q", q=P),
                                   mT[k][2 * ST * side:2 * ST * (side + 1), :], dma_m[buf])
                m_ready[g] = a
                st["m_sent"] = [a]

            def st_step(s):
                g, n = divmod(s, NS)
                c, j = STEPS[n]
                buf = g % NST
                q0 = max(c * BANK, j * P)
                w = (c + 1) * BANK - q0
                pe.wait(m_ready[g])
                for pair in range(2):
                    b0 = STB[pair]
                    pe.wait(*bank_free[b0])
                    for side in range(2):
                        r = slice(64 * side, 64 * side + QR)
                        m = mm(psum[:, b0 + side, 0:w], Ks[buf][r, pair, j * P:(j + 1) * P], Qs[buf][r, pair, q0:q0 + w],
                               True, True, pe_s)
                    slot = 2 * (s % 2) + pair
                    act.wait(m, *st.get(("pv", s - 2), []))
                    e_ = act.do(lambda e, slot=slot, b0=b0: e.activation(pr[:, slot, :, 0:w], psum[:, b0:b0 + 2, 0:w],
                                                                         ACT.Exp, scale=SC1), act_exp)
                    bank_free[b0] = [e_]
                    if j * P >= c * BANK:
                        pool.wait(e_)
                        e_ = pool.do(lambda e, slot=slot: e.affine_select(
                            out=pr[:, slot, :, 0:P], in_=pr[:, slot, :, 0:P], compare_op=ALU.is_ge, fill=0.0, base=0,
                            pattern=[[0, 2], [1, P]], channel_multiplier=-1), pool_mask)
                    st[("pr", s, pair)] = e_
                if n == NS - 1:
                    stack_free[g] = [m]

            def pv_step(s):
                g, n = divmod(s, NS)
                b, gl = divmod(g, G)
                c, j = STEPS[n]
                q0 = max(c * BANK, j * P)
                w = (c + 1) * BANK - q0
                if j == 0:
                    pe.wait(*bank_free[PVB], va_ready[b])
                for pair in range(2):
                    pe.wait(st[("pr", s, pair)])
                for pair in range(2):
                    for side in range(2):
                        head, ct = 8 * pair + 2 * gl + side, 2 * pair + side
                        m = mm(psum[32 * ct:32 * ct + VB, PVB, BANK - w:BANK], va[b % 2][:, j, head * VW:head * VW + VB],
                               pr[:, 2 * (s % 2) + pair, side, 0:w], j == 0, j == 4 * c + 3,
                               pe_pv if pair and side else None)
                st[("pv", s)] = [m]
                if j == 4 * c + 3:
                    dve.wait(m, *st.get("oT", []))
                    o = dve.do(lambda e: e.tensor_copy(oT[:, :], psum[:, PVB, :]), dve_out)
                    bank_free[PVB] = [o]
                    st[("o", g, c)] = o
                    if c == 1 and gl == G - 1:
                        va_free[b % 2] = [m]

            def unturn(g, c):
                b, gl = divmod(g, G)
                pe.wait(*bank_free[SIDE], st[("o", g, c)])
                for t in range(HALF):
                    m = pe.do(lambda e, t=t: e.transpose(psum[:, SIDE, t * P:(t + 1) * P], oT[:, t * P:(t + 1) * P],
                                                         ident[:, :]), pe_tr)
                st["oT"] = [m]
                src = psum[:, SIDE, :].rearrange("p (t h w) -> p t h w", t=HALF, w=VB)
                dve.wait(m)
                r = dve.do(lambda e: e.reciprocal(rd4[:, :].rearrange("p (t h) -> p t h", t=HALF), src[:, :, :, DK]), dve_out)
                dve.wait(r, *st.get(("attn_free", c), []), *free["y"][c])
                o = dve.do(lambda e: e.tensor_tensor(
                    attn[:, HALF * c:HALF * (c + 1), 64 * gl:64 * (gl + 1)].rearrange("p t (h w) -> p t h w", w=DK),
                    src[:, :, :, 0:DK],
                    rd4[:, :].rearrange("p (t h) -> p t h", t=HALF).unsqueeze(3).to_broadcast([P, HALF, 4, DK]), ALU.mult), dve_out)
                bank_free[SIDE] = [o]
                st[("attn", b, c)] = o

            def post3(b):
                def tr(half, c):
                    m, done = transpose_half(SIDE, attn[:, HALF * half:HALF * (half + 1), :], [st[("attn", b, half)]], c,
                                             aT[0][:, c, :], aT[1][:, c, :], st.get("aT_free", []))
                    st[("attn_free", half)] = [m]
                    st["aT"] = done

                def wo(half, t):
                    pe.wait(*bank_free[SIDE], st["aT"])
                    for n in range(2):
                        tok = slice((t + n) * P, (t + n + 1) * P)
                        m = mm_split(psum[:, SIDE, n * D:(n + 1) * D], [((aT[0][:, k, tok], aT[1][:, k, tok]),
                                                                         (wo_hi[:, k, :], wo_lo[:, k, :])) for k in range(KC)],
                                     pe_prod)
                    act.wait(m)
                    o = act.do(lambda e: e.activation(y[:, half, t:t + 2, :],
                                                      psum[:, SIDE, :].rearrange("p (t d) -> p t d", t=2), ACT.Copy), act_out)
                    bank_free[SIDE] = [o]
                    st["aT_free"] = [m]
                    st[("y", half)] = o

                def fin(half):
                    add_out(b, half, [st[("y", half)]])
                return [f for half in range(2) for f in
                        ([lambda half=half, c=c: tr(half, c) for c in range(KC)]
                         + [lambda half=half, t=t: wo(half, t) for t in (0, 2)] + [lambda half=half: fin(half)])]

            for u in pre3(0) + proj3(0):
                u()
            for g in range(3):
                load_stack(g)
            total = B * G * NS
            plan = {}

            def at(s, unit):
                plan.setdefault(s, []).append(unit)
            for g in range(B * G):
                s0 = g * NS
                at(s0 - 3, lambda g=g: put_max(g))
                at(s0 + 8, lambda g=g: unturn(g, 0))
                at(s0 + NS + 1, lambda g=g: unturn(g, 1))
                if g >= 3:
                    at(s0 - 2 * NS, lambda g=g: load_stack(g))
            for b in range(B):
                end = (b + 1) * G * NS
                for n, u in enumerate(post3(b)):
                    at(end + 2 + n, u)
                if b + 1 < B:
                    units = pre3(b + 1) + proj3(b + 1)
                    for n, u in enumerate(units):
                        at(end - 3 * NS - 2 + n, u)
            for s in range(-LEAD, total + 16):
                if s + LEAD < total:
                    max_block(*divmod(s + LEAD, NS))
                if 0 <= s < total:
                    st_step(s)
                for u in plan.get(s, []):
                    u()
                if 0 <= s - 1 < total:
                    pv_step(s - 1)
            barrier()

        with ExitStack() as ph:
            layer3(ph)

        def layer4(ph):
            W = {}
            w_ready = {}
            for n, (name, src, k, cols) in enumerate((("w1", w1T, KC, HID), ("w2", w2T, KC, HID), ("h1", h1T, HC, HID),
                                                      ("h2", h2T, HC, HID), ("w3", w3T, HC, D))):
                W[name] = sb(ph, "W" + name, [P, k, cols])
                w_ready[name] = sp.dma(W[name][:, :, :], rows(src), ld[n])
            sc = {}
            for name, src in (("s1", s1), ("s2", s2), ("h1", sh1), ("h2", sh2)):
                sc[name] = sb(ph, "sc" + name, [P, HC])
                sc_ready = sp.dma(sc[name][:, :], src, ld[5])
            s3b = sb(ph, "s3b", [P, D])
            sc_ready = sp.dma(s3b[:, :], s3.to_broadcast([P, D]), ld[5])
            act.wait(sc_ready)
            dve.wait(sc_ready)
            room_for(ph, 4, 2)
            xn, y = room["xn"], room["y"]
            xT = sb(ph, "xT4", [P, 2, KC, BANK])
            hbuf = [sb(ph, f"h{i}", [P, HC, BANK]) for i in range(2)]
            sil = sb(ph, "sil", [P, 2, BANK])
            xT_free, h_free, sil_free = [[], []], [[], []], [[], []]
            ready = {}

            def pre4(n):
                b, half = divmod(n, 2)
                k = n % 2
                norms = norm_in(b, half)
                for c in range(KC):
                    bank = c
                    pe.wait(*bank_free[bank], *norms)
                    for t in range(HALF):
                        m = pe.do(lambda e, t=t, c=c, bank=bank: e.transpose(psum[:, bank, t * P:(t + 1) * P],
                                                                  xn[:, half, t, c * P:(c + 1) * P], ident[:, :]), pe_tr)
                    act.wait(m, *xT_free[k])
                    o = act.do(lambda e, c=c, bank=bank: e.activation(xT[:, k, c, :], psum[:, bank, :], ACT.Copy), act_hi)
                    bank_free[bank] = [o]
                free["xn"][half] = [m]
                ready[n] = o

            bank_n = [0]

            def next_bank():
                bank_n[0] += 1
                return 2 + bank_n[0] % 6

            def product(bank, w, src, oc):
                pe.wait(*bank_free[bank])
                kk = w.shape[1]
                for c in range(kk):
                    m = mm(psum[:, bank, :], w[:, c, oc * P:(oc + 1) * P], src[:, c, :], c == 0, c == kk - 1,
                           pe_h if c == kk - 1 else None)
                return m

            pre4(0)
            for n in range(2 * B):
                b, half = divmod(n, 2)
                k = n % 2
                pe.wait(ready[n], w_ready["w1"], w_ready["w2"])
                act.wait(*h_free[0])
                for oc in range(HC):
                    ba, bb = next_bank(), next_bank()
                    ma = product(ba, W["w1"], xT[:, k], oc)
                    q = oc % 2
                    act.wait(ma, *sil_free[q])
                    a_ = act.do(lambda e, oc=oc, q=q, ba=ba: e.activation(sil[:, q, :], psum[:, ba, :], ACT.Silu,
                                                                          scale=sc["s1"][:, oc:oc + 1]), act_h)
                    bank_free[ba] = [a_]
                    mb = product(bb, W["w2"], xT[:, k], oc)
                    dve.wait(mb, a_, *h_free[0])
                    d_ = dve.do(lambda e, oc=oc, q=q, bb=bb: e.scalar_tensor_tensor(
                        hbuf[0][:, oc, :], psum[:, bb, :], sc["s2"][:, oc:oc + 1], sil[:, q, :], ALU.mult, ALU.mult), dve_h)
                    bank_free[bb] = [d_]
                    sil_free[q] = [d_]
                xT_free[k] = [mb]
                pe.wait(d_, w_ready["h1"])
                if n + 1 < 2 * B:
                    pre4(n + 1)
                for name, i in (("h1", 0), ("h2", 1)):
                    pe.wait(w_ready[name])
                    for oc in range(HC):
                        bk = next_bank()
                        m = product(bk, W[name], hbuf[i], oc)
                        act.wait(m, *h_free[1 - i])
                        a_ = act.do(lambda e, oc=oc, i=i, bk=bk, name=name: e.activation(
                            hbuf[1 - i][:, oc, :], psum[:, bk, :], ACT.Gelu, scale=sc[name][:, oc:oc + 1]), act_h)
                        bank_free[bk] = [a_]
                    h_free[i] = [m]
                    pe.wait(a_)
                pe.wait(w_ready["w3"])
                dve.wait(*free["y"][half])
                for t in range(HALF):
                    bk = next_bank()
                    pe.wait(*bank_free[bk])
                    for c in range(HC):
                        m = mm(psum[:, bk, 0:D], hbuf[0][:, c, t * P:(t + 1) * P], W["w3"][:, c, :], c == 0, c == HC - 1,
                               pe_h if c == HC - 1 else None)
                    dve.wait(m)
                    o = dve.do(lambda e, t=t, half=half, bk=bk: e.tensor_tensor(y[:, half, t, :], psum[:, bk, 0:D], s3b[:, :],
                                                                                ALU.mult), dve_out)
                    bank_free[bk] = [o]
                h_free[0] = [m]
                done = add_out(b, half, [o])
                sp.wait(done)
                last = sp.dma(out[b].rearrange("(t p) d -> p t d", p=P)[:, HALF * half:HALF * (half + 1), :],
                              x[:, b * ST + half * HALF:b * ST + (half + 1) * HALF, :], st_out)
            sp.wait(last)

        with ExitStack() as ph:
            layer4(ph)

        block = ctx.enter_context(nc.Block())
        block.tensor(lambda e: pe.emit(e))
        block.scalar(lambda e: act.emit(e))
        block.vector(lambda e: dve.emit(e))
        block.gpsimd(lambda e: pool.emit(e))
        block.sync(lambda e: sp.emit(e))


def kernel(**inputs):
    import concourse.bacc as bacc
    from concourse.bass_utils import run_bass_kernel_spmd as run

    a = {k: np.asarray(v) for k, v in inputs.items()}
    wo = a["L1_attn_w_o"].T.reshape(2, 4, 2, DK, D).transpose(1, 0, 2, 3, 4).reshape(D, D)
    laid = {
        "x": a["L0_attn_x"], "wq0": a["L0_attn_Wq"], "wk0": a["L0_attn_Wk"], "wv0": a["L0_attn_Wv"],
        "theta": a["L0_ffn_theta"], "phi": a["L0_ffn_phi"], "theta_n": a["L0_ffn_theta_noise"],
        "phi_n": a["L0_ffn_phi_noise"], "wqkvT": a["L1_attn_w_qkv"].reshape(3 * D, D).T, "woT": wo,
        "w1T": a["L1_ffn_w1_w"].T, "w2T": a["L1_ffn_w2_w"].T, "h1T": a["L1_ffn_h1_w"].T, "h2T": a["L1_ffn_h2_w"].T,
        "w3T": a["L1_ffn_w3_w"].T,
        "s1": a["L1_ffn_w1_s"].reshape(HC, P).T, "s2": a["L1_ffn_w2_s"].reshape(HC, P).T,
        "sh1": a["L1_ffn_h1_s"].reshape(HC, P).T, "sh2": a["L1_ffn_h2_s"].reshape(HC, P).T,
        "s3": a["L1_ffn_w3_s"].reshape(1, D),
    }
    nc = bacc.Bacc("TRN2", target_bir_lowering=False, num_devices=1)
    arrays, args = {}, []
    for name, v in laid.items():
        v = np.ascontiguousarray(v)
        arrays[f"in_{name}"] = v
        args.append(nc.dram_tensor(f"in_{name}", v.shape, mybir.dt.from_np(v.dtype), kind="ExternalInput").ap())
    args.append(nc.dram_tensor("out_x", (B, S, D), f32, kind="ExternalOutput").ap())
    sandwich(nc, *args)
    r = run(nc, [arrays], core_ids=[0])
    return r.results[0]["out_x"]
```

```python
from contextlib import ExitStack

import concourse.bass as bass
import numpy as np
from concourse import mybir

B, S, D = 4, 1024, 256
HID = 1024
H, DK = 16, 16
P = 128
BANK = 512
KC = D // P
HC = HID // P
ST = S // P
HALF = 4
NT = B * ST
EPS = 1e-5
NEG = -3.0e38

f32 = mybir.dt.float32
f32r = mybir.dt.float32r
bf16 = mybir.dt.bfloat16
ALU = mybir.AluOpType
ACT = mybir.ActivationFunctionType
AX = mybir.AxisListType


class Signal:

    def __init__(self, sem):
        self.sem, self.value = sem, 0


class Engine:

    def __init__(self):
        self.queue, self.waited = [], {}

    def wait(self, *marks):
        for mark in marks:
            if mark is None:
                continue
            signal, value = mark
            if self.waited.get(signal, 0) < value:
                self.waited[signal] = value
                self.queue.append(lambda e, s=signal.sem, v=value: e.wait_ge(s, v))

    def do(self, op, signal=None, by=1):
        if signal is None:
            self.queue.append(op)
            return None
        signal.value += by
        self.queue.append(lambda e: op(e).then_inc(signal.sem, by))
        return signal, signal.value

    def dma(self, out, in_, signal):
        in_ = in_.bitcast(f32) if in_.dtype == f32r else in_
        return self.do(lambda e: e.dma_start(out, in_), signal, 16)

    def branch(self, flag, taken, other):
        def op(e):
            value = e.value_load(flag, min_val=0, max_val=1)
            with e.If(value):
                for o in taken:
                    o(e)
            with e.Else():
                for o in other:
                    o(e)
        self.queue.append(op)

    def emit(self, e):
        for op in self.queue:
            op(e)


def sandwich(nc, x_in, wq0, wk0, wv0, theta, phi, theta_n, phi_n, wqkvT, woT, w1T, w2T, h1T, h2T,
             w3T, s1, s2, sh1, sh2, s3, out):
    pe, act, dve, pool, sp = (Engine() for _ in range(5))
    engines = (pe, act, dve, pool, sp)
    ctx = ExitStack()
    with ctx:
        signals = []

        def signal(name):
            signals.append(Signal(ctx.enter_context(nc.semaphore(name))))
            return signals[-1]

        def sb(where, name, shape, dt=f32):
            return where.enter_context(nc.sbuf_tensor(name, shape, dt))

        psum = ctx.enter_context(nc.psum_tensor("psum", [P, 8, BANK], f32))
        bank_free = [[] for _ in range(8)]

        def mm(o, l, r, start, stop, done=None):
            return pe.do(lambda e: e.matmul(o, l, r, start=start, stop=stop), done)

        def plain(ap):
            return ap.bitcast(f32)

        ld = [signal(f"ld{i}") for i in range(6)]
        ld_x = [signal(f"ld_x{b}") for b in range(B)]
        pool_const = signal("pool_const")
        dve_stat = signal("dve_stat")
        act_std = signal("act_std")
        dve_norm = signal("dve_norm")
        pool_res = signal("pool_res")
        pe_tr = signal("pe_tr")
        act_hi = signal("act_hi")
        dve_lo = signal("dve_lo")
        pe_prod = signal("pe_prod")
        act_out = signal("act_out")
        dve_out = signal("dve_out")
        pe_s = signal("pe_s")
        pe_pv = signal("pe_pv")
        dve_max = signal("dve_max")
        act_exp = signal("act_exp")
        pool_mask = signal("pool_mask")
        pe_max = signal("pe_max")
        dve_m = signal("dve_m")
        act_m = signal("act_m")
        pe_m = signal("pe_m")
        dma_m = [signal(f"dma_m{i}") for i in range(3)]
        dma_stack = [signal(f"dma_stack{i}") for i in range(3)]
        dve_w = signal("dve_w")
        act_w = signal("act_w")
        pe_h = signal("pe_h")
        act_h = signal("act_h")
        dve_h = signal("dve_h")
        ld_w = [signal(f"ld_w{i}") for i in range(10)]
        st_x = signal("st_x")
        st_out = signal("st_out")
        ld_a = [signal(f"ld_a{i}") for i in range(2)]
        ld_r = signal("ld_r")
        ld_c = [signal(f"ld_c{i}") for i in range(2)]
        act_c = signal("act_c")
        dve_c = signal("dve_c")
        act_raw = signal("act_raw")

        def barrier():
            for e in engines:
                e.wait(*[(s, s.value) for s in signals if s.value])
            for marks in bank_free:
                marks.clear()

        ident = sb(ctx, "ident", [P, P])
        ident16 = sb(ctx, "ident16", [P, P], bf16)
        tri16 = sb(ctx, "tri16", [P, P], bf16)
        eps = sb(ctx, "eps", [P, 1])
        one = sb(ctx, "one", [P, 1])
        flag = sb(ctx, "flag", [1, 1], mybir.dt.int32)
        room = {}
        moments = {}
        for way in ("in", "out"):
            moments[way] = (sb(ctx, f"stat_{way}", [P, HALF, 6]), sb(ctx, f"mv_{way}", [P, HALF, 2]),
                            sb(ctx, f"std_{way}", [P, HALF]), sb(ctx, f"rstd_{way}", [P, HALF]))
        early = ctx.enter_context(ExitStack())
        x = sb(early, "x", [P, NT, D])
        trig = [sb(early, "trig_hi", [P, KC, 2 * D], f32r), sb(early, "trig_lo", [P, KC, 2 * D], f32r)]
        xs = nc.dram_tensor("x_stream", (B, S, D), f32).ap()
        xs_ready = {}

        def half_of(ap, b, half):
            return ap[b].rearrange("(t p) d -> p t d", p=P)[:, HALF * half:HALF * (half + 1), :]

        x_ready = []

        def load_x(b):
            x_ready.extend([sp.dma(x[:, b * ST:(b + 1) * ST, :], x_in[b].rearrange("(t p) d -> p t d", p=P), ld_x[b])] * ST)

        load_x(0)

        c = [pool.do(lambda e: e.memset(ident[:, :], 0.0), pool_const),
             pool.do(lambda e: e.memset(ident16[:, :], 0.0), pool_const),
             pool.do(lambda e: e.memset(tri16[:, :], 0.0), pool_const),
             pool.do(lambda e: e.memset(one[:, :], 1.0), pool_const),
             pool.do(lambda e: e.memset(eps[:, :], EPS), pool_const)]
        pool.wait(c[-1])
        for t in (ident, ident16):
            pool.do(lambda e, t=t: e.affine_select(out=t[:, :], in_=t[:, :], compare_op=ALU.not_equal, fill=1.0,
                                                   base=0, pattern=[[-1, P]], channel_multiplier=1), pool_const)
        const_ready = pool.do(lambda e: e.affine_select(out=tri16[:, :], in_=tri16[:, :], compare_op=ALU.is_ge,
                                                        fill=NEG, base=0, pattern=[[-1, P]],
                                                        channel_multiplier=1), pool_const)
        act.wait(const_ready)
        pe.wait(const_ready)

        free = {"xn": [[], []], "y": [[], []]}

        def norm_a(way, src, ready):
            stat, mv, std, _ = moments[way]
            dve.wait(*ready, *free[way])
            for t in range(HALF):
                m = dve.do(lambda e, t=t: e.bn_stats(stat[:, t, :], src(t)), dve_stat)
            for t in range(HALF):
                dve.wait((dve_stat, m[1] - HALF + 1 + t))
                v = dve.do(lambda e, t=t: e.bn_aggr(mv[:, t, :], stat[:, t, :]), dve_stat)
            act.wait(v)
            return act.do(lambda e: e.activation(std[:, :], mv[:, :, 1], ACT.Sqrt, bias=eps[:, :]), act_std)

        def norm_b(way, std_ready, src, dst, before=()):
            _, mv, std, rstd = moments[way]
            dve.wait(std_ready)
            m = dve.do(lambda e: e.reciprocal(rstd[:, :], std[:, :]), dve_stat)
            dve.wait(m, *before)
            for t in range(HALF):
                m = dve.do(lambda e, t=t: e.tensor_scalar(dst(t), src(t), mv[:, t, 0:1], rstd[:, t:t + 1],
                                                          ALU.subtract, ALU.mult), dve_norm)
            free[way] = [m]
            return m

        free["in"], free["out"] = [], []

        def room_for(where, layer, n_xn, n_y, y=None):
            room["xn"] = sb(where, f"xn{layer}", [P, n_xn, HALF, D])
            room["y"] = sb(where, f"y{layer}", [P, n_y, HALF, D]) if y is None else y
            free["xn"], free["y"] = [[] for _ in range(n_xn)], [[] for _ in range(n_y)]

        def norm_in(b, half, src, ready):
            xn, n = room["xn"], len(free["xn"])
            k, done = half % n, {}

            def a():
                done["std"] = norm_a("in", lambda t: src[:, t, :], ready() if callable(ready) else ready)

            def b_():
                done["xn"] = norm_b("in", done["std"], lambda t: src[:, t, :], lambda t: xn[:, k, t, :], free["xn"][k])
            return a, b_, done

        def add_out(half, y_ready, dst, dst_ready, then):
            y, k, done = room["y"], half % len(free["y"]), {}

            def a():
                done["std"] = norm_a("out", lambda t: y[:, k, t, :], y_ready())

            def b_():
                m = norm_b("out", done["std"], lambda t: y[:, k, t, :], lambda t: y[:, k, t, :])
                pool.wait(m, *dst_ready())
                m = pool.do(lambda e: e.tensor_tensor(dst, dst, y[:, k, :, :], ALU.add), pool_res)
                free["y"][k] = [m]
                then(m)
            return a, b_

        def evac_split(bank, src, hi, lo, before=()):
            act.wait(*before)
            h = act.do(lambda e: e.activation(hi, src, ACT.Copy), act_hi)
            dve.wait(*before)
            dve.wait(h)
            m = dve.do(lambda e: e.tensor_tensor(lo, src, plain(hi), ALU.subtract), dve_lo)
            bank_free[bank] = [m]
            return m

        def transpose_half(bank, src, ready, c, hi, lo, wait_free):
            pe.wait(*bank_free[bank], ready)
            for t in range(HALF):
                m = pe.do(lambda e, t=t: e.transpose(psum[:, bank, t * P:(t + 1) * P],
                                                     src[:, t, c * P:(c + 1) * P], ident[:, :]),
                          pe_tr if t == HALF - 1 else None)
            act.wait(m)
            return m, evac_split(bank, psum[:, bank, :], hi, lo, wait_free)

        def mm_split(o, terms, done, start=True, stop=True):
            ops = [p for (lh, ll), (rh, rl) in terms for p in ((lh, rh), (lh, rl), (ll, rh))]
            for n, (l, r) in enumerate(ops):
                last = n == len(ops) - 1
                m = mm(o, l, r, start and n == 0, stop and last, done if last else None)
            return m

        def split_weight(where, name, src, shape, raw, sig):
            hi, lo = sb(where, name + "_hi", shape, f32r), sb(where, name + "_lo", shape, f32r)
            raw = raw.rearrange("p (c n) -> p c n", c=shape[1])
            m = sp.dma(raw, src, sig)
            act.wait(m)
            h = act.do(lambda e: e.activation(hi[:, :, :], raw, ACT.Copy), act_w)
            dve.wait(m, h)
            return (hi, lo), dve.do(lambda e: e.tensor_tensor(lo[:, :, :], raw, plain(hi[:, :, :]), ALU.subtract), dve_w)

        def rows(w):
            return w.rearrange("(c p) n -> p c n", p=P)

        def spread(units, steps):
            n = len(units)
            return [units[n * i // steps:n * (i + 1) // steps] for i in range(steps)]

        TWO_PI = 2 * np.pi
        C1 = 6.28125
        C2 = float(np.float32(TWO_PI - C1))
        C3 = float(TWO_PI - C1 - C2)
        PI_BELOW = float(np.nextafter(np.float32(np.pi), np.float32(0)))
        ROUND = 1.5 * 2.0 ** 23

        def trig_half(n, w, w_noise, ang, noise, turns):
            sp.dma(ang.rearrange("p (c d) -> p c d", c=KC), rows(w), ld[4])
            a = sp.dma(noise.rearrange("p (c d) -> p c d", c=KC), rows(w_noise), ld[4])
            dve.wait(a)
            quarter, shift = (0.25, float(np.pi / 2)) if n == 0 else (0.0, 0.0)
            steps = [lambda e: e.tensor_tensor(ang, ang, noise, ALU.add),
                     lambda e: e.tensor_scalar(turns, ang, 1 / TWO_PI, quarter, ALU.mult, ALU.add),
                     lambda e: e.tensor_scalar(turns, turns, ROUND, None, ALU.add),
                     lambda e: e.tensor_scalar(turns, turns, -ROUND, None, ALU.add)]
            steps += [lambda e, c=c: e.scalar_tensor_tensor(ang, turns, -c, ang, ALU.mult, ALU.add) for c in (C1, C2, C3)]
            steps += [lambda e: e.tensor_scalar(ang, ang, shift, PI_BELOW, ALU.add, ALU.min),
                      lambda e: e.tensor_scalar(ang, ang, -PI_BELOW, None, ALU.max)]
            for op in steps:
                m = dve.do(op, dve_w)
                dve.wait(m)
            act.wait(m)
            m = act.do(lambda e: e.activation(ang, ang, ACT.Sin), act_w)
            act.wait(m)
            hi, lo = (t[:, :, n * D:(n + 1) * D] for t in trig)
            wave = ang.rearrange("p (c d) -> p c d", c=KC)
            m = act.do(lambda e: e.activation(hi, wave, ACT.Copy), act_w)
            dve.wait(m)
            return dve.do(lambda e: e.tensor_tensor(lo, wave, plain(hi), ALU.subtract), dve_w)

        def trig_weights(scratch):
            areas = [scratch[:, i, :] for i in range(3)]
            m = trig_half(0, theta, theta_n, *areas)
            sp.wait(m)
            return trig_half(1, phi, phi_n, *areas)

        PIECE = 512
        pieces = [(name, w, c, o, min(PIECE, w.shape[1])) for name, w in
                  (("w1", w1T), ("w2", w2T), ("h1", h1T), ("h2", h2T), ("w3", w3T))
                  for c in range(w.shape[0] // P) for o in range(0, w.shape[1], PIECE)]
        changed = sb(early, "changed", [P, len(pieces)])
        counted = []

        def round_unit(raw, hi, n):
            name, w, c, o, cols = pieces[n]
            k = n % 2
            r, h = raw[:, k, 0:cols], hi[:, k, 0:cols]
            sp.wait(free.get(("raw", k)))
            m = sp.dma(r, w[c * P:(c + 1) * P, o:o + cols], ld_c[k])
            act.wait(m)
            a = act.do(lambda e: e.activation(h, r, ACT.Copy), act_c)
            dve.wait(m, a)
            d = dve.do(lambda e: e.scalar_tensor_tensor(r, r, 1.0, plain(h), ALU.mult, ALU.not_equal,
                                                        accum_out=changed[:, n:n + 1]), dve_c)
            free[("raw", k)] = d
            if n == len(pieces) - 1:
                counted.append(d)

        SC0 = 1.0 / D ** 0.5
        def layer1(ph):
            room_for(ph, 1, 1, 2)
            xn, y = room["xn"], room["y"]
            flat_y = y[:, :, :, :].rearrange("p h t d -> p (h t d)")
            wts = []
            for n, w in enumerate((wq0, wk0, wv0)):
                t, w_ready = split_weight(ph, f"w0{n}", rows(w), [P, KC, D], flat_y[:, n * KC * D:(n + 1) * KC * D], ld[n])
                wts.append(t)
            pe.wait(w_ready)
            for b in range(1, B):
                load_x(b)
            xT = [sb(ph, f"xT0_{k}", [P, KC, S], f32r) for k in ("hi", "lo")]
            qT = [[sb(ph, f"qT{i}_{k}", [P, KC, S], f32r) for k in ("hi", "lo")] for i in range(2)]
            kT = [[sb(ph, f"kT{i}_{k}", [P, KC, S], f32r) for k in ("hi", "lo")] for i in range(2)]
            v = [[sb(ph, f"v{i}_{k}", [P, ST, D], f32r) for k in ("hi", "lo")] for i in range(2)]
            raw = sb(ph, "raw", [P, 2, PIECE])
            raw_hi = sb(ph, "raw_hi", [P, 2, PIECE], f32r)
            prob = sb(ph, "prob", [P, 2, S])
            pT = [sb(ph, f"pT_{k}", [P, ST, P], f32r) for k in ("hi", "lo")]
            mx = sb(ph, "mx0", [P, 2])
            nb = sb(ph, "nb0", [P, 2])
            den = sb(ph, "den0", [P, 2])
            rden = sb(ph, "rden0", [P, 2])
            xT_free, qkv_free = [], [[], []]
            ring = [4]

            def next_bank():
                ring[0] = ring[0] + 1 if ring[0] < 7 else 4
                return ring[0]

            def pre_units(b):
                def tr(half, c, done):
                    cols = slice(half * BANK, (half + 1) * BANK)
                    m, mark = transpose_half(next_bank(), xn[:, 0, :, :], done["xn"], c, xT[0][:, c, cols], xT[1][:, c, cols],
                                             xT_free)
                    free["xn"][0] = [m]
                    xT_ready[(b, half)] = mark
                units = []
                for half in range(2):
                    t0 = b * ST + HALF * half
                    a, b_, done = norm_in(b, half, x[:, t0:t0 + HALF, :], x_ready[t0:t0 + HALF])
                    units += [a, b_, lambda half=half, done=done: tr(half, 0, done), lambda half=half, done=done: tr(half, 1, done)]
                return units

            def proj_units(b):
                def qk(dst, w, c, half):
                    SIDE = next_bank()
                    pe.wait(*bank_free[SIDE], xT_ready[(b, half)])
                    cols = slice(half * BANK, (half + 1) * BANK)
                    m = mm_split(psum[:, SIDE, :], [((w[0][:, k, c * P:(c + 1) * P], w[1][:, k, c * P:(c + 1) * P]),
                                                     (xT[0][:, k, cols], xT[1][:, k, cols])) for k in range(KC)], pe_prod)
                    act.wait(m)
                    qkv_ready[b] = evac_split(SIDE, psum[:, SIDE, :], dst[0][:, c, cols], dst[1][:, c, cols], qkv_free[b % 2])
                    return m

                def val(t):
                    SIDE = next_bank()
                    pe.wait(*bank_free[SIDE], xT_ready[(b, 1)])
                    w = wts[2]
                    for n in range(2):
                        tok = slice((t + n) * P, (t + n + 1) * P)
                        m = mm_split(psum[:, SIDE, n * D:(n + 1) * D], [((xT[0][:, k, tok], xT[1][:, k, tok]),
                                                                         (w[0][:, k, :], w[1][:, k, :])) for k in range(KC)],
                                     pe_prod)
                    act.wait(m)
                    qkv_ready[b] = evac_split(SIDE, psum[:, SIDE, :].rearrange("p (t d) -> p t d", t=2),
                                              v[b % 2][0][:, t:t + 2, :], v[b % 2][1][:, t:t + 2, :], qkv_free[b % 2])
                    xT_free[:] = [m]
                return ([lambda c=c, half=half, dst=dst, w=w: qk(dst, w, c, half)
                         for half in range(2) for dst, w in ((qT[b % 2], wts[0]), (kT[b % 2], wts[1])) for c in range(KC)]
                        + [lambda t=t: val(t) for t in range(0, ST, 2)])

            xT_ready, qkv_ready = {}, {}
            y_ready = {}
            st = {}

            def scores(b, i):
                n, Q, K = b * ST + i, qT[b % 2], kT[b % 2]
                k = n % 2
                pair = (2 * k, 2 * k + 1)
                pe.wait(*bank_free[pair[0]], qkv_ready[b])
                tok = slice(i * P, (i + 1) * P)
                w_all = (i + 1) * P
                for c0 in range(0, w_all, BANK):
                    w = min(BANK, w_all - c0)
                    mm_split(psum[:, pair[c0 // BANK], 0:w],
                             [((Q[0][:, kk, tok], Q[1][:, kk, tok]), (K[0][:, kk, c0:c0 + w], K[1][:, kk, c0:c0 + w]))
                              for kk in range(KC)], None, stop=c0 + w < w_all)
                d = i * P % BANK
                m = mm(psum[:, pair[i * P // BANK], d:d + P], ident16[:, :], tri16[:, :], False, True, pe_s)
                src = psum[:, pair[0]:pair[0] + 2, :].rearrange("p a n -> p (a n)")[:, 0:w_all]
                dve.wait(m, *st.get(("exp", n - 2), []))
                a = dve.do(lambda e: e.tensor_reduce(mx[:, k:k + 1], src, AX.X, ALU.max), dve_max)
                dve.wait(a)
                a = dve.do(lambda e: e.tensor_scalar(nb[:, k:k + 1], mx[:, k:k + 1], -SC0, None, ALU.mult), dve_max)
                st[("nb", n)] = a

            def exps(b, i):
                n = b * ST + i
                k = n % 2
                w_all = (i + 1) * P
                pair = (2 * k, 2 * k + 1)
                src = psum[:, pair[0]:pair[0] + 2, :].rearrange("p a n -> p (a n)")[:, 0:w_all]
                act.wait(st[("nb", n)], *st.get(("pT", n - 2), []), *st.get(("rden", n - 2), []))
                ex = act.do(lambda e: e.activation(prob[:, k, 0:w_all], src, ACT.Exp, bias=nb[:, k:k + 1], scale=SC0,
                                                   accum_out=den[:, k:k + 1]), act_exp)
                bank_free[pair[0]] = bank_free[pair[1]] = [ex]
                st[("exp", n)] = [ex]

            def turn(b, i):
                n = b * ST + i
                k = n % 2
                pe.wait(*st[("exp", n)])
                dve.wait(*st[("exp", n)])
                rd = dve.do(lambda e: e.reciprocal(rden[:, k:k + 1], den[:, k:k + 1]), dve_max)
                st[("rden", n)] = [rd]
                for k0 in range(0, i + 1, 4):
                    kk = min(4, i + 1 - k0)
                    bank = next_bank()
                    pe.wait(*bank_free[bank])
                    for j in range(kk):
                        m = pe.do(lambda e, j=j, bank=bank, k0=k0: e.transpose(psum[:, bank, j * P:(j + 1) * P],
                                                                  prob[:, k, (k0 + j) * P:(k0 + j + 1) * P], ident[:, :]),
                                  pe_tr)
                    act.wait(m)
                    st[("pTr", n)] = [evac_split(bank, psum[:, bank, 0:kk * P].rearrange("p (k q) -> p k q", q=P),
                                                 pT[0][:, k0:k0 + kk, :], pT[1][:, k0:k0 + kk, :],
                                                 st.get(("pv", n - 1), []))]
                st[("pT", n)] = [m]

            def weigh(b, i):
                n, V, O = b * ST + i, v[b % 2], next_bank()
                half, t = i // HALF, i % HALF
                pe.wait(*st[("pTr", n)], *bank_free[O])
                m = mm_split(psum[:, O, 0:D], [((pT[0][:, j, :], pT[1][:, j, :]), (V[0][:, j, :], V[1][:, j, :]))
                                               for j in range(i + 1)], pe_pv)
                st[("pv", n)] = [m]
                act.wait(m, *st[("rden", n)], *free["y"][half])
                o = act.do(lambda e: e.activation(y[:, half, t, :], psum[:, O, 0:D], ACT.Copy,
                                                  scale=rden[:, n % 2:n % 2 + 1]), act_out)
                st[("rden", n)] = [o]
                bank_free[O] = [o]
                if i == ST - 1:
                    qkv_free[b % 2] = [m]
                if t == HALF - 1:
                    t0 = b * ST + HALF * half

                    def then(m):
                        x_ready[t0:t0 + HALF] = [m] * HALF
                    out_units.extend(add_out(half, lambda: [o], x[:, t0:t0 + HALF, :], lambda: x_ready[t0:t0 + 1], then))

            out_units = []
            for u in pre_units(0) + proj_units(0):
                u()
            sp.wait(w_ready)
            trig_ready = trig_weights(flat_y.rearrange("p (i n) -> p i n", i=4))
            free["y"] = [[trig_ready], [trig_ready]]
            for b in range(B):
                side = spread(pre_units(b + 1) + proj_units(b + 1) if b + 1 < B else [], ST)
                for i in range(ST):
                    n = b * ST + i
                    scores(b, i)
                    if n >= 1:
                        turn(*divmod(n - 1, ST))
                    exps(b, i)
                    for u in side[i]:
                        u()
                    if n >= 1:
                        weigh(*divmod(n - 1, ST))
                    if out_units:
                        out_units.pop(0)()
                    round_unit(raw, raw_hi, n)
            turn(B - 1, ST - 1)
            weigh(B - 1, ST - 1)
            for u in out_units:
                u()
            barrier()

        with ExitStack() as ph:
            layer1(ph)

        def layer2(ph):
            room_for(ph, 2, 2, 2)
            xn, y = room["xn"], room["y"]
            xT = [[sb(ph, f"xT1_{i}{k}", [P, KC, BANK], f32r) for k in ("hi", "lo")] for i in range(2)]
            sq = sb(ph, "sq", [P, 2, 2 * D])
            pw = sb(ph, "pw", [P, 2, HALF, D])
            raw = sb(ph, "raw2", [P, 2, PIECE])
            raw_hi = sb(ph, "raw_hi2", [P, 2, PIECE], f32r)
            cnt = sb(ph, "cnt", [P, 1])
            xT_free = [[], []]
            sq_free, pw_free = [[], []], [[], []]
            ready, outs = {}, []
            ring = [0]

            def next_bank():
                ring[0] = (ring[0] + 1) % 8
                return ring[0]

            def pre_half(n):
                half, t0, k = n % 2, n * HALF, n % 2
                a, b_, done = norm_in(n // 2, half, x[:, t0:t0 + HALF, :], x_ready[t0:t0 + HALF])

                def tr(c):
                    m, ready[n] = transpose_half(next_bank(), xn[:, half, :, :], done["xn"], c, xT[k][0][:, c, :],
                                                 xT[k][1][:, c, :], xT_free[k])
                    free["xn"][half] = [m]
                return [a, b_, lambda: tr(0), lambda: tr(1)]

            def tile(n, t):
                k, q, bank = n % 2, t % 2, next_bank()
                pe.wait(*bank_free[bank], ready[n])
                tok = slice(t * P, (t + 1) * P)
                m = mm_split(psum[:, bank, :], [((xT[k][0][:, c, tok], xT[k][1][:, c, tok]),
                                                 (trig[0][:, c, :], trig[1][:, c, :])) for c in range(KC)], pe_prod)
                act.wait(m, *sq_free[q])
                s_ = act.do(lambda e: e.activation(sq[:, q, :], psum[:, bank, :], ACT.Square), act_h)
                bank_free[bank] = [s_]
                dve.wait(s_, *pw_free[k])
                d_ = dve.do(lambda e: e.tensor_tensor(pw[:, k, t, :], sq[:, q, 0:D], sq[:, q, D:2 * D], ALU.add), dve_h)
                sq_free[q] = [d_]
                xT_free[k] = [m]
                return d_

            def root(n, d_):
                half, k, t0 = n % 2, n % 2, n * HALF
                act.wait(d_, *free["y"][half])
                o = act.do(lambda e: e.activation(y[:, half, :, :], pw[:, k, :, :], ACT.Sqrt), act_out)
                pw_free[k] = [o]

                def then(m):
                    sp.wait(m)
                    xs_ready[(n // 2, half)] = sp.dma(half_of(xs, n // 2, half), x[:, t0:t0 + HALF, :], st_x)
                outs.extend(add_out(half, lambda: [o], x[:, t0:t0 + HALF, :], lambda: x_ready[t0:t0 + 1], then))

            n_round = NT
            for u in pre_half(0):
                u()
            for n in range(2 * B):
                pre = pre_half(n + 1) if n + 1 < 2 * B else [lambda: None] * 4
                for t in range(HALF):
                    d_ = tile(n, t)
                    pre[t]()
                    if outs:
                        outs.pop(0)()
                    if n_round < len(pieces):
                        round_unit(raw, raw_hi, n_round)
                        n_round += 1
                root(n, d_)
            for u in outs:
                u()
            while n_round < len(pieces):
                round_unit(raw, raw_hi, n_round)
                n_round += 1
            dve.wait(*counted)
            m = dve.do(lambda e: e.tensor_reduce(cnt[:, :], changed[:, :], AX.X, ALU.add), dve_c)
            pe.wait(m, *bank_free[0])
            m = pe.do(lambda e: e.matmul(psum[0:1, 0, 0:1], cnt[:, :], one[:, :], start=True, stop=True), pe_m)
            dve.wait(m)
            m = dve.do(lambda e: e.tensor_scalar(flag[:, :], psum[0:1, 0, 0:1], 0.0, None, ALU.is_gt), dve_c)
            bank_free[0] = [m]
            barrier()

        with ExitStack() as ph:
            layer2(ph)
        early.close()

        G = 4
        SC1 = 1.0 / DK ** 0.5
        NST = 3
        STEPS = [(c, j) for c in range(S // BANK) for j in range(4 * (c + 1))]
        NS = len(STEPS)
        LEAD = NS + 3
        KR = 3 * DK
        def layer3(ph):
            attn = sb(ph, "attn", [P, ST, D])
            flat = attn[:, :, :].rearrange("p t d -> p (t d)")
            (wa_hi, wa_lo), m1 = split_weight(ph, "wqkv", rows(wqkvT), [P, KC, 3 * D], flat[:, 0:KC * 3 * D], ld[0])
            (wo_hi, wo_lo), m2 = split_weight(ph, "wo", rows(woT), [P, KC, D], flat[:, KC * 3 * D:], ld[1])
            xT = [sb(ph, f"xT2_{k}", [P, KC, S], f32r) for k in ("hi", "lo")]
            nat = {"q": [sb(ph, f"q_{k}", [P, 2, S], f32r) for k in ("hi", "lo")],
                   "k": [sb(ph, f"k_{k}", [P, 2, S], f32r) for k in ("hi", "lo")]}
            VW = DK + 1
            VB = 2 * DK
            va = [sb(ph, f"va{i}", [P, ST, H * VW + VB - VW]) for i in range(2)]
            Qs = [sb(ph, f"Qs{i}", [P, 2, S], f32r) for i in range(NST)]
            Ks = [sb(ph, f"Ks{i}", [P, 2, 2, S], f32r) for i in range(NST)]
            pr = sb(ph, "pr", [P, 4, 2, BANK])
            maskw = sb(ph, "maskw", [P, BANK])
            mxs = sb(ph, "mxs", [P, 2, 2, 2, ST])
            mT = [sb(ph, f"mT_{k}", [2 * 2 * ST, P], f32r) for k in ("hi", "lo")]
            oT = sb(ph, "oT", [P, BANK])
            room_for(ph, 3, 1, 2, attn[:, :, :].rearrange("p (h t) d -> p h t d", h=2))
            xn, y = room["xn"], room["y"]
            aT = [sb(ph, f"aT_{k}", [P, KC, 2 * P], f32r) for k in ("hi", "lo")]
            xa = sb(ph, "xa3", [P, HALF, D])
            xr = sb(ph, "xr3", [P, HALF, D])
            junk = sb(ph, "junk", [P, 2, BANK], bf16)
            rd4 = sb(ph, "rd4", [P, HALF * 4])

            m = pool.do(lambda e: e.memset(maskw[:, :], 0.0), pool_const)
            pool.wait(m)
            pool.do(lambda e: e.affine_select(out=maskw[:, BANK - P:], in_=maskw[:, BANK - P:], compare_op=ALU.is_ge,
                                              fill=NEG, base=0, pattern=[[-1, P]], channel_multiplier=1), pool_const)
            for i in range(2):
                pool.do(lambda e, i=i: e.memset(va[i][:, :, :], 1.0), pool_const)
            for i in range(NST):
                pool.do(lambda e, i=i: e.memset(Qs[i][:, :, :].bitcast(f32), 0.0), pool_const)
                zero = pool.do(lambda e, i=i: e.memset(Ks[i][:, :, :, :].bitcast(f32), 0.0), pool_const)
            dve.wait(zero)
            for i in range(NST):
                for side in range(2):
                    ones = dve.do(lambda e, i=i, side=side: e.memset(
                        Ks[i][64 * side + 32:64 * side + 64, side, :, :].bitcast(f32), 1.0), dve_w)
            pe.wait(ones)
            sp.wait(ones)
            init_ready = zero
            for e in (pe, dve, act, sp):
                e.wait(init_ready)
            pe.wait(m1, m2)

            MAXB, SIDE, STB, PVB = (0, 1), 2, (3, 5), 7
            xT_free, nat_free, va_free = [], [], [[], []]
            xT_ready, nat_ready, va_ready = {}, {}, {}
            stack_ready, stack_free = {}, {}
            m_ready, max_done = {}, {}
            st = {}

            def pre3(b):
                def load(half):
                    sp.wait(xs_ready[(b, half)], *st.get("xa_free", []))
                    st["xa"] = sp.dma(xa[:, :, :], half_of(xs, b, half), ld_a[0])

                def tr(half, c, done):
                    cols = slice(half * BANK, (half + 1) * BANK)
                    st["xa_free"] = [done["xn"]]
                    m, mark = transpose_half(SIDE, xn[:, 0, :, :], done["xn"], c, xT[0][:, c, cols], xT[1][:, c, cols],
                                             xT_free)
                    free["xn"][0] = [m]
                    xT_ready[(b, half)] = mark
                units = []
                for half in range(2):
                    a, b_, done = norm_in(b, half, xa, lambda: [st["xa"]])
                    units += [lambda half=half: load(half), a, b_,
                              lambda half=half, done=done: tr(half, 0, done), lambda half=half, done=done: tr(half, 1, done)]
                return units

            def proj3(b):
                def qk(name, c, half):
                    o = (0 if name == "q" else D) + c * P
                    cols = slice(half * BANK, (half + 1) * BANK)
                    pe.wait(*bank_free[SIDE], xT_ready[(b, half)])
                    m = mm_split(psum[:, SIDE, :], [((wa_hi[:, k, o:o + P], wa_lo[:, k, o:o + P]),
                                                     (xT[0][:, k, cols], xT[1][:, k, cols])) for k in range(KC)], pe_prod)
                    act.wait(m)
                    hi, lo = nat[name]
                    nat_ready[b] = evac_split(SIDE, psum[:, SIDE, :], hi[:, c, cols], lo[:, c, cols], nat_free)

                def val(t):
                    pe.wait(*bank_free[SIDE], xT_ready[(b, 1)])
                    for n in range(2):
                        tok = slice((t + n) * P, (t + n + 1) * P)
                        m = mm_split(psum[:, SIDE, n * D:(n + 1) * D],
                                     [((xT[0][:, k, tok], xT[1][:, k, tok]), (wa_hi[:, k, 2 * D:], wa_lo[:, k, 2 * D:]))
                                      for k in range(KC)], pe_prod)
                    act.wait(m, *va_free[b % 2])
                    for n in range(2):
                        dst = va[b % 2][:, t + n, 0:H * VW].rearrange("p (h w) -> p h w", w=VW)[:, :, 0:DK]
                        o = act.do(lambda e, n=n, dst=dst: e.activation(
                            dst, psum[:, SIDE, n * D:(n + 1) * D].rearrange("p (h w) -> p h w", w=DK), ACT.Copy), act_out)
                    bank_free[SIDE] = [o]
                    va_ready[b] = o
                    xT_free[:] = [m]
                return ([lambda name=name, c=c, half=half: qk(name, c, half)
                         for half in range(2) for name in "qk" for c in range(2)]
                        + [lambda t=t: val(t) for t in range(0, ST, 2)])

            def load_stack(g):
                b, gl = divmod(g, G)
                i = g % NST
                pool.wait(nat_ready[b], *stack_free.get(g - NST, []))
                for side in range(2):
                    d = 64 * side + KR
                    pool.dma(Qs[i][d:d + 2, :, :], Qs[i][d + 2:d + 4, :, :], dma_stack[i])
                    r = 32 * gl + DK * side
                    for k, (q_, k_) in enumerate(((0, 0), (1, 0), (0, 1))):
                        d = 64 * side + DK * k
                        pool.dma(Qs[i][d:d + DK, :, :], nat["q"][q_][r:r + DK, :, :], dma_stack[i])
                        m = pool.dma(Ks[i][d:d + DK, side, :, :], nat["k"][k_][r:r + DK, :, :], dma_stack[i])
                stack_ready[g] = m
                if gl == G - 1:
                    nat_free[:] = [stack_ready[g - n] for n in range(G)]

            max_blocks = [(i, k0, min(BANK, (i + 1) * P - k0)) for i in range(ST) for k0 in range(0, (i + 1) * P, BANK)]
            count = {"max": 0}

            def max_unit(g, n, pair, side):
                i, k0, w = max_blocks[n]
                buf, mb = g % NST, g % 2
                diag = k0 + w == (i + 1) * P
                if n == 0:
                    dve.wait(*st.get(("mread", g - 2), []))
                bank = MAXB[count["max"] % 2]
                jk = count["max"] % 2
                count["max"] += 1
                pe.wait(stack_ready[g], *bank_free[bank])
                m = mm(psum[:, bank, 0:w], Qs[buf][:, pair, i * P:(i + 1) * P], Ks[buf][:, side, pair, k0:k0 + w],
                       True, True, pe_max)
                dst = mxs[:, mb, side, pair, i:i + 1]
                dve.wait(m)
                if not diag:
                    a = dve.do(lambda e: e.tensor_reduce(dst, psum[:, bank, 0:w], AX.X, ALU.max), dve_max)
                    st[("part", side, pair)] = a
                else:
                    first = NEG
                    if k0:
                        dve.wait(st[("part", side, pair)])
                        first = dst
                    dve.wait(*st.get(("junk", jk), []))
                    a = dve.do(lambda e: e.tensor_tensor_reduce(
                        out=junk[:, jk, 0:w], in0=psum[:, bank, 0:w], in1=maskw[:, BANK - w:], scale=1.0, scalar=first,
                        op0=ALU.add, op1=ALU.max, accum_out=dst), dve_max)
                    st[("junk", jk)] = [a]
                bank_free[bank] = [a]
                st[("mx", g)] = a

            def put_max(g):
                buf, mb = g % NST, g % 2
                n = 2 * 2 * ST
                pe.wait(*bank_free[SIDE], st[("mx", g)])
                m = pe.do(lambda e: e.transpose(psum[0:n, SIDE, 0:P], mxs[:, mb, :, :, :].rearrange("p s a t -> p (s a t)"),
                                                ident[:, :]), pe_m)
                st[("mread", g)] = [m]
                act.wait(m, *st.get("m_sent", []))
                dve.wait(*st.get("m_sent", []))
                h = act.do(lambda e: e.activation(mT[0][:, :], psum[0:n, SIDE, 0:P], ACT.Copy, scale=-1.0), act_m)
                dve.wait(h)
                l = dve.do(lambda e: e.scalar_tensor_tensor(mT[1][:, :], psum[0:n, SIDE, 0:P], -1.0, plain(mT[0][:, :]),
                                                            ALU.mult, ALU.subtract), dve_m)
                bank_free[SIDE] = [l]
                pool.wait(h, l)
                for side in range(2):
                    for k in range(2):
                        d = 64 * side + KR + k
                        a = pool.dma(Qs[buf][d:d + 1, :, :].rearrange("o a (t q) -> o (a t) q", q=P),
                                   mT[k][2 * ST * side:2 * ST * (side + 1), :], dma_m[buf])
                m_ready[g] = a
                st["m_sent"] = [a]

            def st_pair(s, pair):
                g, n = divmod(s, NS)
                c, j = STEPS[n]
                buf = g % NST
                q0 = max(c * BANK, j * P)
                w = (c + 1) * BANK - q0
                b0 = STB[pair]
                slot = 2 * (s % 2) + pair
                pe.wait(m_ready[g], *bank_free[b0])
                for side in range(2):
                    m = mm(psum[:, b0 + side, 0:w], Ks[buf][:, side, pair, j * P:(j + 1) * P], Qs[buf][:, pair, q0:q0 + w],
                           True, True, pe_s)
                act.wait(m, *st.get(("pv", s - 2), []))
                e_ = act.do(lambda e: e.activation(pr[:, slot, :, 0:w], psum[:, b0:b0 + 2, 0:w], ACT.Exp, scale=SC1), act_exp)
                bank_free[b0] = [e_]
                if j * P >= c * BANK:
                    pool.wait(e_)
                    e_ = pool.do(lambda e: e.affine_select(
                        out=pr[:, slot, :, 0:P], in_=pr[:, slot, :, 0:P], compare_op=ALU.is_ge, fill=0.0, base=0,
                        pattern=[[0, 2], [1, P]], channel_multiplier=-1), pool_mask)
                st[("pr", s, pair)] = e_
                if n == NS - 1:
                    stack_free[g] = [m]

            def pv_step(s):
                g, n = divmod(s, NS)
                b, gl = divmod(g, G)
                c, j = STEPS[n]
                q0 = max(c * BANK, j * P)
                w = (c + 1) * BANK - q0
                if j == 0:
                    pe.wait(*bank_free[PVB], va_ready[b])
                for pair in range(2):
                    pe.wait(st[("pr", s, pair)])
                for pair in range(2):
                    for side in range(2):
                        head, ct = 8 * pair + 2 * gl + side, 2 * pair + side
                        m = mm(psum[32 * ct:32 * ct + VB, PVB, BANK - w:BANK], va[b % 2][:, j, head * VW:head * VW + VB],
                               pr[:, 2 * (s % 2) + pair, side, 0:w], j == 0, j == 4 * c + 3,
                               pe_pv if pair and side else None)
                st[("pv", s)] = [m]
                if j == 4 * c + 3:
                    dve.wait(m, *st.get("oT", []))
                    o = dve.do(lambda e: e.tensor_copy(oT[:, :], psum[:, PVB, :]), dve_out)
                    bank_free[PVB] = [o]
                    st[("o", g, c)] = o
                    if c == 1 and gl == G - 1:
                        va_free[b % 2] = [m]

            def unturn(g, c):
                b, gl = divmod(g, G)
                pe.wait(*bank_free[SIDE], st[("o", g, c)])
                for t in range(HALF):
                    m = pe.do(lambda e, t=t: e.transpose(psum[:, SIDE, t * P:(t + 1) * P], oT[:, t * P:(t + 1) * P],
                                                         ident[:, :]), pe_tr)
                st["oT"] = [m]
                src = psum[:, SIDE, :].rearrange("p (t h w) -> p t h w", t=HALF, w=VB)
                dve.wait(m)
                r = dve.do(lambda e: e.reciprocal(rd4[:, :].rearrange("p (t h) -> p t h", t=HALF), src[:, :, :, DK]), dve_out)
                dve.wait(r, *st.get(("attn_free", c), []), *free["y"][c])
                o = dve.do(lambda e: e.tensor_tensor(
                    attn[:, HALF * c:HALF * (c + 1), 64 * gl:64 * (gl + 1)].rearrange("p t (h w) -> p t h w", w=DK),
                    src[:, :, :, 0:DK],
                    rd4[:, :].rearrange("p (t h) -> p t h", t=HALF).unsqueeze(3).to_broadcast([P, HALF, 4, DK]), ALU.mult), dve_out)
                bank_free[SIDE] = [o]
                st[("attn", b, c)] = o

            def post3(b):
                def load(half):
                    sp.wait(xs_ready[(b, half)], *st.get("xr_free", []))
                    st["xr"] = sp.dma(xr[:, :, :], half_of(xs, b, half), ld_r)

                def tr(half, t):
                    pe.wait(*bank_free[SIDE], st[("attn", b, half)])
                    for c in range(KC):
                        for n in range(2):
                            m = pe.do(lambda e, c=c, n=n: e.transpose(
                                psum[:, SIDE, (2 * c + n) * P:(2 * c + n + 1) * P],
                                attn[:, HALF * half + t + n, c * P:(c + 1) * P], ident[:, :]),
                                pe_tr if c == KC - 1 and n == 1 else None)
                    act.wait(m)
                    st["aT"] = evac_split(SIDE, psum[:, SIDE, :].rearrange("p (c t) -> p c t", c=KC),
                                          aT[0][:, :, :], aT[1][:, :, :], st.get("aT_free", []))

                def wo(half, t):
                    pe.wait(*bank_free[SIDE], st["aT"])
                    for n in range(2):
                        tok = slice(n * P, (n + 1) * P)
                        m = mm_split(psum[:, SIDE, n * D:(n + 1) * D], [((aT[0][:, k, tok], aT[1][:, k, tok]),
                                                                         (wo_hi[:, k, :], wo_lo[:, k, :])) for k in range(KC)],
                                     pe_prod)
                    act.wait(m)
                    o = act.do(lambda e: e.activation(y[:, half, t:t + 2, :],
                                                      psum[:, SIDE, :].rearrange("p (t d) -> p t d", t=2), ACT.Copy), act_out)
                    bank_free[SIDE] = [o]
                    st["aT_free"] = [m]
                    st[("y", half)] = o

                def then(half, m):
                    sp.wait(m)
                    xs_ready[(b, half)] = sp.dma(half_of(xs, b, half), xr[:, :, :], st_x)
                    st["xr_free"] = [xs_ready[(b, half)]]
                units = []
                for half in range(2):
                    units += [lambda half=half: (load(half), tr(half, 0)), lambda half=half: wo(half, 0),
                              lambda half=half: tr(half, 2), lambda half=half: wo(half, 2),
                              *add_out(half, lambda half=half: [st[("y", half)]], xr[:, :, :], lambda: [st["xr"]],
                                       lambda m, half=half: then(half, m))]
                return units

            for u in pre3(0) + proj3(0):
                u()
            for g in range(3):
                load_stack(g)
            total = B * G * NS
            plan = {}

            def at(s, unit):
                plan.setdefault(s, []).append(unit)
            for b in range(B):
                end = (b + 1) * G * NS
                for n, u in enumerate(post3(b)):
                    at(end + 2 + n, u)
                if b + 1 < B:
                    units = pre3(b + 1) + proj3(b + 1)
                    for n, u in enumerate(units):
                        at(end - 3 * NS - 8 + n, u)
            for g in range(B * G):
                s0 = g * NS
                at(s0 - 3, lambda g=g: put_max(g))
                at(s0 + 9, lambda g=g: unturn(g, 0))
                at(s0 + NS + 1, lambda g=g: unturn(g, 1))
                if g >= 3:
                    at(s0 - 2 * NS, lambda g=g: load_stack(g))
            for s in range(-LEAD, total + 16):
                mx = [lambda p=p, side=side: max_unit(*divmod(s + LEAD, NS), p, side) for p in range(2) for side in range(2)]
                if s + LEAD >= total:
                    mx = []
                stp = [lambda p=p: st_pair(s, p) for p in range(2)] if 0 <= s < total else []
                pv = [lambda: pv_step(s - 1)] if 0 <= s - 1 < total else []
                for u in mx[0:1] + stp[0:1] + mx[1:2] + stp[1:2] + mx[2:3] + pv + mx[3:4] + plan.get(s, []):
                    u()
            barrier()

        with ExitStack() as ph:
            layer3(ph)

        def layer4(ph, fast):
            parts = ("hi", "lo") if fast else ("all",)
            dt = f32r if fast else f32
            tag = "f" if fast else "g"
            src = {"w1": w1T, "w2": w2T, "h1": h1T, "h2": h2T, "w3": w3T}
            loader = pool if fast else sp
            W, w_ready = {}, {}
            room_for(ph, 4 if fast else 5, 1, 1)
            xn, y = room["xn"], room["y"]
            xa = sb(ph, "xa" + tag, [P, 2, HALF, D])
            xa_ready, xa_free = {}, [[], []]

            def load_x(n):
                k = n % 2
                sp.wait(xs_ready[divmod(n, 2)], *xa_free[k])
                xa_ready[n] = sp.dma(xa[:, k, :, :], half_of(xs, *divmod(n, 2)), ld_a[k])

            load_x(0)
            sc = {}
            for name, vec in (("s1", s1), ("s2", s2), ("h1", sh1), ("h2", sh2)):
                sc[name] = sb(ph, tag + "sc" + name, [P, HC])
                sp.dma(sc[name][:, :], vec, ld[5])
            s3b = sb(ph, tag + "s3b", [P, D])
            sc_ready = sp.dma(s3b[:, :], s3.to_broadcast([P, D]), ld[5])
            for n, name in enumerate(("w1", "w2", "h1", "h2", "w3")):
                k, cols = src[name].shape[0] // P, src[name].shape[1]
                W[name] = sb(ph, tag + "W" + name, [P, k, cols], dt)
                for c in range(k):
                    w_ready[(name, c)] = loader.dma(W[name][:, c, :], src[name][c * P:(c + 1) * P, :], ld_w[5 * (not fast) + n])
            for name in ("w1", "w2", "h1", "h2", "w3"):
                for c in range(W[name].shape[1]):
                    w_ready[(name, c)] = w_ready[(name, W[name].shape[1] - 1)]
            act.wait(sc_ready)
            dve.wait(sc_ready)
            xT = {k: sb(ph, f"{tag}xT_{k}", [P, 2, KC, BANK], dt) for k in parts}
            hid = [{k: sb(ph, f"{tag}h{i}_{k}", [P, HC, BANK], dt) for k in parts} for i in range(2)]
            sil = sb(ph, tag + "sil", [P, 2, BANK])
            act_raw_buf = sb(ph, tag + "raw", [P, 2, BANK])
            xT_free, h_free, sil_free, raw_free = [[], []], [[], []], [[], []], [[], []]
            xT_ready, h_ready = {}, [{}, {}]
            bank_n, raw_n = [0], [0]

            def next_bank():
                bank_n[0] = (bank_n[0] + 1) % 8
                return bank_n[0]

            def views(buf, *at):
                return [buf[k][at] for k in parts]

            def product(o, bank, w, chunks, moving, ready, name):
                pe.wait(*bank_free[bank])
                ops = [(c, part) for c in range(chunks) for part in range(len(parts))]
                for n, (c, part) in enumerate(ops):
                    pe.wait(ready(c), w_ready[(name, c)])
                    last = n == len(ops) - 1
                    l, r = (w(c), moving[1](c)[part]) if moving[0] else (moving[1](c)[part], w(c))
                    m = mm(o, l, r, n == 0, last, pe_h if last else None)
                return m

            def pre4(n):
                k = n % 2
                a, b_, done = norm_in(n // 2, n % 2, xa[:, k, :, :], lambda: [xa_ready[n]])

                def tr(c):
                    bank = next_bank()
                    if fast:
                        m, mark = transpose_half(bank, xn[:, 0, :, :], done["xn"], c, xT["hi"][:, k, c, :],
                                                 xT["lo"][:, k, c, :], xT_free[k])
                    else:
                        pe.wait(*bank_free[bank], done["xn"])
                        for t in range(HALF):
                            m = pe.do(lambda e, t=t: e.transpose(psum[:, bank, t * P:(t + 1) * P],
                                                                 xn[:, 0, t, c * P:(c + 1) * P], ident[:, :]), pe_tr)
                        act.wait(m, *xT_free[k])
                        mark = act.do(lambda e: e.activation(xT["all"][:, k, c, :], psum[:, bank, :], ACT.Copy), act_hi)
                        bank_free[bank] = [mark]
                    free["xn"][0] = [m]
                    xT_ready[(n, c)] = mark
                return [a, b_, lambda: tr(0), lambda: tr(1)]

            def keep(i, oc, raw, mark):
                if not fast:
                    return
                hi, lo = hid[i]["hi"][:, oc, :], hid[i]["lo"][:, oc, :]
                act.wait(mark, *h_free[i])
                h = act.do(lambda e: e.activation(hi, raw, ACT.Copy), act_hi)
                dve.wait(mark, h, *h_free[i])
                h_ready[i][oc] = dve.do(lambda e: e.tensor_tensor(lo, raw, plain(hi), ALU.subtract), dve_lo)

            def target(i, oc):
                if not fast:
                    return hid[i]["all"][:, oc, :], h_free[i], None
                k = raw_n[0] % 2
                raw_n[0] += 1
                return act_raw_buf[:, k, :], raw_free[k], k

            def gated(n, oc):
                k, q = n % 2, oc % 2
                ba, bb = next_bank(), next_bank()
                cols = slice(oc * P, (oc + 1) * P)
                moving = (True, lambda c: views(xT, slice(None), k, c, slice(None)))
                ma = product(psum[:, ba, :], ba, lambda c: W["w1"][:, c, cols], KC, moving, lambda c: xT_ready[(n, c)], "w1")
                act.wait(ma, *sil_free[q])
                a_ = act.do(lambda e: e.activation(sil[:, q, :], psum[:, ba, :], ACT.Silu, scale=sc["s1"][:, oc:oc + 1]), act_h)
                bank_free[ba] = [a_]
                mb = product(psum[:, bb, :], bb, lambda c: W["w2"][:, c, cols], KC, moving, lambda c: xT_ready[(n, c)], "w2")
                dst, dst_free, r_ = target(0, oc)
                dve.wait(mb, a_, *dst_free)
                d_ = dve.do(lambda e: e.scalar_tensor_tensor(dst, psum[:, bb, :], sc["s2"][:, oc:oc + 1], sil[:, q, :],
                                                             ALU.mult, ALU.mult), dve_h)
                bank_free[bb], sil_free[q] = [d_], [d_]
                h_ready[0][oc] = d_
                keep(0, oc, dst, d_)
                if fast:
                    raw_free[r_] = [h_ready[0][oc]]
                xT_free[k] = [mb]

            def dense(i, name, oc):
                bk = next_bank()
                cols = slice(oc * P, (oc + 1) * P)
                m = product(psum[:, bk, :], bk, lambda c: W[name][:, c, cols], HC,
                            (True, lambda c: views(hid[i], slice(None), c, slice(None))), lambda c: h_ready[i][c], name)
                dst, dst_free, r_ = target(1 - i, oc)
                act.wait(m, *dst_free)
                a_ = act.do(lambda e: e.activation(dst, psum[:, bk, :], ACT.Gelu, scale=sc[name][:, oc:oc + 1]), act_raw)
                bank_free[bk] = [a_]
                h_ready[1 - i][oc] = a_
                keep(1 - i, oc, dst, a_)
                if fast:
                    raw_free[r_] = [h_ready[1 - i][oc]]
                if oc == HC - 1:
                    h_free[i] = [m]

            def last_product(n, t):
                bk = next_bank()
                m = product(psum[:, bk, 0:D], bk, lambda c: W["w3"][:, c, :], HC,
                            (False, lambda c: views(hid[0], slice(None), c, slice(t * P, (t + 1) * P))),
                            lambda c: h_ready[0][c], "w3")
                dve.wait(m, *free["y"][0])
                o = dve.do(lambda e: e.tensor_tensor(y[:, 0, t, :], psum[:, bk, 0:D], s3b[:, :], ALU.mult), dve_out)
                bank_free[bk] = [o]
                h_free[0] = [m]
                return o

            def finish(n, o):
                b, half = divmod(n, 2)
                k = n % 2

                def then(m):
                    sp.wait(m)
                    xa_free[k] = [sp.dma(half_of(out, b, half), xa[:, k, :, :], st_out)]
                return list(add_out(half, lambda: [o], xa[:, k, :, :], lambda: [], then))

            for u in pre4(0):
                u()
            outs = []
            for n in range(2 * B):
                pre = []
                if n + 1 < 2 * B:
                    pre = pre4(n + 1)
                for oc in range(HC):
                    gated(n, oc)
                    if outs and oc >= 1:
                        outs.pop(0)()
                if n + 1 < 2 * B:
                    load_x(n + 1)
                for oc in range(HC):
                    dense(0, "h1", oc)
                for oc in range(HC):
                    dense(1, "h2", oc)
                    if pre and oc >= 2:
                        pre.pop(0)()
                for t in range(HALF):
                    o = last_product(n, t)
                outs = finish(n, o)
            for u in outs:
                u()
            sp.wait(xa_free[0][0], xa_free[1][0])

        for e in engines:
            e.before, e.queue = e.queue, []
        values, waited = [s.value for s in signals], [dict(e.waited) for e in engines]
        forms = []
        for fast in (False, True):
            for s, v in zip(signals, values):
                s.value = v
            for e, w in zip(engines, waited):
                e.waited, e.queue = dict(w), []
            free["in"], free["out"] = [], []
            for marks in bank_free:
                marks.clear()
            with ExitStack() as ph:
                layer4(ph, fast)
            forms.append([e.queue for e in engines])
        for e, general, quick in zip(engines, *forms):
            e.queue = e.before
            e.branch(flag[0:1, 0:1], general, quick)

        block = ctx.enter_context(nc.Block())
        block.tensor(lambda e: pe.emit(e))
        block.scalar(lambda e: act.emit(e))
        block.vector(lambda e: dve.emit(e))
        block.gpsimd(lambda e: pool.emit(e))
        block.sync(lambda e: sp.emit(e))


def kernel(**inputs):
    import concourse.bacc as bacc
    from concourse.bass_utils import run_bass_kernel_spmd as run

    a = {k: np.asarray(v) for k, v in inputs.items()}
    wo = a["L1_attn_w_o"].T.reshape(2, 4, 2, DK, D).transpose(1, 0, 2, 3, 4).reshape(D, D)
    laid = {
        "x": a["L0_attn_x"], "wq0": a["L0_attn_Wq"], "wk0": a["L0_attn_Wk"], "wv0": a["L0_attn_Wv"],
        "theta": a["L0_ffn_theta"], "phi": a["L0_ffn_phi"], "theta_n": a["L0_ffn_theta_noise"],
        "phi_n": a["L0_ffn_phi_noise"], "wqkvT": a["L1_attn_w_qkv"].reshape(3 * D, D).T, "woT": wo,
        "w1T": a["L1_ffn_w1_w"].T, "w2T": a["L1_ffn_w2_w"].T, "h1T": a["L1_ffn_h1_w"].T, "h2T": a["L1_ffn_h2_w"].T,
        "w3T": a["L1_ffn_w3_w"].T,
        "s1": a["L1_ffn_w1_s"].reshape(HC, P).T, "s2": a["L1_ffn_w2_s"].reshape(HC, P).T,
        "sh1": a["L1_ffn_h1_s"].reshape(HC, P).T, "sh2": a["L1_ffn_h2_s"].reshape(HC, P).T,
        "s3": a["L1_ffn_w3_s"].reshape(1, D),
    }
    nc = bacc.Bacc("TRN2", target_bir_lowering=False, num_devices=1)
    arrays, args = {}, []
    for name, v in laid.items():
        v = np.ascontiguousarray(v)
        arrays[f"in_{name}"] = v
        args.append(nc.dram_tensor(f"in_{name}", v.shape, mybir.dt.from_np(v.dtype), kind="ExternalInput").ap())
    args.append(nc.dram_tensor("out_x", (B, S, D), f32, kind="ExternalOutput").ap())
    sandwich(nc, *args)
    r = run(nc, [arrays], core_ids=[0])
    return r.results[0]["out_x"]
```

```python
from contextlib import ExitStack

import concourse.bass as bass
import numpy as np
from concourse import mybir

B, S, D = 4, 1024, 256
HID = 1024
H, DK = 16, 16
P = 128
BANK = 512
KC = D // P
HC = HID // P
ST = S // P
HALF = 4
NT = B * ST
EPS = 1e-5
NEG = -3.0e38

f32 = mybir.dt.float32
f32r = mybir.dt.float32r
bf16 = mybir.dt.bfloat16
ALU = mybir.AluOpType
ACT = mybir.ActivationFunctionType
AX = mybir.AxisListType
i32 = mybir.dt.int32
RSQRT_GUESS = float(0x5F3759DF)


class Signal:

    def __init__(self, sem):
        self.sem, self.value = sem, 0


class Engine:

    def __init__(self):
        self.queue, self.waited = [], {}

    def wait(self, *marks):
        for mark in marks:
            if mark is None:
                continue
            signal, value = mark
            if self.waited.get(signal, 0) < value:
                self.waited[signal] = value
                self.queue.append(lambda e, s=signal.sem, v=value: e.wait_ge(s, v))

    def do(self, op, signal=None, by=1):
        if signal is None:
            self.queue.append(op)
            return None
        signal.value += by
        self.queue.append(lambda e: op(e).then_inc(signal.sem, by))
        return signal, signal.value

    def dma(self, out, in_, signal):
        in_ = in_.bitcast(f32) if in_.dtype == f32r else in_
        return self.do(lambda e: e.dma_start(out, in_), signal, 16)

    def branch(self, flag, taken, other):
        def op(e):
            value = e.value_load(flag, min_val=0, max_val=1)
            with e.If(value):
                for o in taken:
                    o(e)
            with e.Else():
                for o in other:
                    o(e)
        self.queue.append(op)

    def emit(self, e):
        for op in self.queue:
            op(e)


def sandwich(nc, x_in, wq0, wk0, wv0, theta, phi, theta_n, phi_n, wqkvT, woT, w1T, w2T, h1T, h2T,
             w3T, s1, s2, sh1, sh2, s3, out):
    pe, act, dve, pool, sp = (Engine() for _ in range(5))
    engines = (pe, act, dve, pool, sp)
    ctx = ExitStack()
    with ctx:
        signals = []

        def signal(name):
            signals.append(Signal(ctx.enter_context(nc.semaphore(name))))
            return signals[-1]

        def sb(where, name, shape, dt=f32):
            return where.enter_context(nc.sbuf_tensor(name, shape, dt))

        psum = ctx.enter_context(nc.psum_tensor("psum", [P, 8, BANK], f32))
        bank_free = [[] for _ in range(8)]

        def mm(o, l, r, start, stop, done=None):
            return pe.do(lambda e: e.matmul(o, l, r, start=start, stop=stop), done)

        def plain(ap):
            return ap.bitcast(f32)

        ld = [signal(f"ld{i}") for i in range(6)]
        ld_x = [signal(f"ld_x{n}") for n in range(2 * B)]
        pool_const = signal("pool_const")
        dve_stat = signal("dve_stat")
        pool_rstd = signal("pool_rstd")
        act_std = signal("act_std")
        act_norm = signal("act_norm")
        dve_norm = signal("dve_norm")
        pool_res = signal("pool_res")
        pe_tr = signal("pe_tr")
        act_hi = signal("act_hi")
        dve_lo = signal("dve_lo")
        pe_prod = signal("pe_prod")
        act_out = signal("act_out")
        dve_out = signal("dve_out")
        pe_s = signal("pe_s")
        pe_pv = signal("pe_pv")
        dve_max = signal("dve_max")
        act_exp = signal("act_exp")
        pe_max = signal("pe_max")
        dve_m = signal("dve_m")
        act_m = signal("act_m")
        pe_m = signal("pe_m")
        dma_m = [signal(f"dma_m{i}") for i in range(3)]
        dma_stack = [signal(f"dma_stack{i}") for i in range(3)]
        act_stack = signal("act_stack")
        pool_stack = signal("pool_stack")
        dve_w = signal("dve_w")
        act_w = signal("act_w")
        pe_h = signal("pe_h")
        act_h = signal("act_h")
        dve_h = signal("dve_h")
        ld_w = [signal(f"ld_w{i}") for i in range(10)]
        st_x = signal("st_x")
        st_out = [signal(f"st_out{i}") for i in range(3)]
        ld_a = [signal(f"ld_a{i}") for i in range(3)]
        ld_r = signal("ld_r")
        ld_c = [signal(f"ld_c{i}") for i in range(4)]
        act_c = signal("act_c")
        dve_c = signal("dve_c")
        act_raw = signal("act_raw")

        def barrier():
            for e in engines:
                e.wait(*[(s, s.value) for s in signals if s.value])
            for marks in bank_free:
                marks.clear()

        ident = sb(ctx, "ident", [P, P])
        ident16 = sb(ctx, "ident16", [P, P], bf16)
        tri16 = sb(ctx, "tri16", [P, P], bf16)
        one = sb(ctx, "one", [P, 1])
        flag = sb(ctx, "flag", [1, 1], i32)
        eps = sb(ctx, "eps", [P, 1])
        room = {"roots": False, "apply": {"in": dve, "out": dve}}
        moments = {}
        for way in ("in", "out"):
            moments[way] = (sb(ctx, f"stat_{way}", [P, HALF, 6]), sb(ctx, f"mv_{way}", [P, HALF, 2]),
                            sb(ctx, f"var_{way}", [P, HALF]), sb(ctx, f"rstd_{way}", [P, HALF]),
                            sb(ctx, f"term_{way}", [P, HALF]))
        shared_xn = sb(ctx, "shared_xn", [P, 1, HALF, D])
        early = ctx.enter_context(ExitStack())
        x = sb(early, "x", [P, NT, D])
        trig = [sb(early, "trig_hi", [P, KC, 2 * D], f32r), sb(early, "trig_lo", [P, KC, 2 * D], f32r)]
        xs = nc.dram_tensor("x_stream", (B, S, D), f32).ap()
        xs_ready = {}

        def half_of(ap, b, half):
            return ap[b].rearrange("(t p) d -> p t d", p=P)[:, HALF * half:HALF * (half + 1), :]

        x_ready = []

        def load_x(n):
            x_ready.extend([sp.dma(x[:, n * HALF:(n + 1) * HALF, :], half_of(x_in, *divmod(n, 2)), ld_x[n])] * HALF)

        load_x(0)

        c = [pool.do(lambda e: e.memset(ident[:, :], 0.0), pool_const),
             pool.do(lambda e: e.memset(ident16[:, :], 0.0), pool_const),
             pool.do(lambda e: e.memset(tri16[:, :], 0.0), pool_const),
             pool.do(lambda e: e.memset(one[:, :], 1.0), pool_const),
             pool.do(lambda e: e.memset(eps[:, :], EPS), pool_const)]
        pool.wait(c[-1])
        for t in (ident, ident16):
            pool.do(lambda e, t=t: e.affine_select(out=t[:, :], in_=t[:, :], compare_op=ALU.not_equal, fill=1.0,
                                                   base=0, pattern=[[-1, P]], channel_multiplier=1), pool_const)
        const_ready = pool.do(lambda e: e.affine_select(out=tri16[:, :], in_=tri16[:, :], compare_op=ALU.is_ge,
                                                        fill=NEG, base=0, pattern=[[-1, P]],
                                                        channel_multiplier=1), pool_const)
        act.wait(const_ready)
        pe.wait(const_ready)

        free = {"xn": [[], []], "y": [[], []]}

        def norm_stats(way, src, ready, tiles):
            stat, mv, var, rstd, term = moments[way]
            dve.wait(*ready, *free[way])
            for t in tiles:
                m = dve.do(lambda e, t=t: e.bn_stats(stat[:, t, :], src(t)), dve_stat)
            for t in tiles:
                dve.wait((dve_stat, m[1] - tiles[-1] + t))
                v = dve.do(lambda e, t=t: e.bn_aggr(mv[:, t, :], stat[:, t, :]), dve_stat)
            if tiles[-1] < HALF - 1:
                return None
            if room["roots"]:
                act.wait(v)
                v = act.do(lambda e: e.activation(var[:, :], mv[:, :, 1], ACT.Sqrt, bias=eps[:, :]), act_std)
                dve.wait(v)
                m = dve.do(lambda e: e.reciprocal(rstd[:, :], var[:, :]), dve_stat)
                dve.wait(m)
                return dve.do(lambda e: e.scalar_tensor_tensor(term[:, :], mv[:, :, 0], -1.0, rstd[:, :],
                                                               ALU.mult, ALU.mult), dve_stat)
            dve.wait(v)
            v = dve.do(lambda e: e.tensor_scalar(var[:, :], mv[:, :, 1], EPS, None, ALU.add), dve_stat)
            dve.wait(v)
            m = dve.do(lambda e: e.tensor_scalar(term[:, :].bitcast(i32), var[:, :].bitcast(i32), 1, None,
                                                 ALU.logical_shift_right), dve_stat)
            dve.wait(m)
            m = dve.do(lambda e: e.tensor_scalar(rstd[:, :].bitcast(i32), term[:, :].bitcast(i32), -1.0, RSQRT_GUESS,
                                                 ALU.mult, ALU.add), dve_stat)
            pool.wait(m)
            for _ in range(3):
                for op in (lambda e: e.tensor_tensor(term[:, :], rstd[:, :], rstd[:, :], ALU.mult),
                           lambda e: e.tensor_tensor(term[:, :], term[:, :], var[:, :], ALU.mult),
                           lambda e: e.tensor_scalar(term[:, :], term[:, :], -0.5, 1.5, ALU.mult, ALU.add),
                           lambda e: e.tensor_tensor(rstd[:, :], rstd[:, :], term[:, :], ALU.mult)):
                    m = pool.do(op, pool_rstd)
                    pool.wait(m)
            return m

        def norm_apply(way, rstd_ready, src, dst, tiles, before=()):
            _, mv, _, rstd, term = moments[way]
            by = room["apply"][way]
            by.wait(rstd_ready, *before)
            for t in tiles:
                if by is act:
                    m = act.do(lambda e, t=t: e.activation(dst(t), src(t), ACT.Identity, bias=term[:, t:t + 1],
                                                           scale=rstd[:, t:t + 1]), act_norm)
                else:
                    m = dve.do(lambda e, t=t: e.tensor_scalar(dst(t), src(t), mv[:, t, 0:1], rstd[:, t:t + 1],
                                                              ALU.subtract, ALU.mult), dve_norm)
            if tiles[-1] == HALF - 1:
                free[way] = [m]
            return m

        free["in"], free["out"] = [], []

        def room_for(where, layer, n_xn, n_y, y=None):
            room["xn"] = sb(where, f"xn{layer}", [P, n_xn, HALF, D]) if n_xn else None
            room["y"] = sb(where, f"y{layer}", [P, n_y, HALF, D]) if y is None else y
            free["xn"], free["y"] = [[] for _ in range(n_xn)], [[] for _ in range(n_y)]

        def norm_in(b, half, src, ready, parts=1):
            xn, n = room["xn"], len(free["xn"])
            k, done = half % n, {}

            def stats(tiles):
                done["rstd"] = norm_stats("in", lambda t: src[:, t, :], ready() if callable(ready) else ready, tiles)

            def apply(tiles):
                done["xn"] = norm_apply("in", done["rstd"], lambda t: src[:, t, :], lambda t: xn[:, k, t, :], tiles,
                                        free["xn"][k])
            return [lambda tiles=tiles, f=f: f(tiles) for f in (stats, apply) for tiles in tiles_of(parts)], done

        def tiles_of(parts):
            return [list(range(HALF * n // parts, HALF * (n + 1) // parts)) for n in range(parts)]

        def add_out(half, y_ready, dst, dst_ready, then, parts=1):
            y, k, done = room["y"], half % len(free["y"]), {}

            def stats(tiles):
                done["rstd"] = norm_stats("out", lambda t: y[:, k, t, :], y_ready(), tiles)

            def apply(tiles):
                m = norm_apply("out", done["rstd"], lambda t: y[:, k, t, :], lambda t: y[:, k, t, :], tiles)
                if tiles[-1] == HALF - 1:
                    pool.wait(m, *dst_ready())
                    m = pool.do(lambda e: e.tensor_tensor(dst, dst, y[:, k, :, :], ALU.add), pool_res)
                    free["y"][k] = [m]
                    then(m)
            return [lambda tiles=tiles, f=f: f(tiles) for f in (stats, apply) for tiles in tiles_of(parts)]

        def evac_split(bank, src, hi, lo, before=(), then=None, late=None):
            act.wait(*before)
            h = act.do(lambda e: e.activation(hi, src, ACT.Copy), act_hi)
            before = tuple(before)

            def lower():
                dve.wait(h, *before)
                m = dve.do(lambda e: e.tensor_tensor(lo, src, plain(hi), ALU.subtract), dve_lo)
                bank_free[bank] = [m]
                if then:
                    then(m)
                return m
            if late is None:
                return lower()
            late.append(lower)

        def transpose_half(bank, src, ready, c, hi, lo, wait_free, *then):
            pe.wait(*bank_free[bank], ready)
            for t in range(HALF):
                m = pe.do(lambda e, t=t: e.transpose(psum[:, bank, t * P:(t + 1) * P],
                                                     src[:, t, c * P:(c + 1) * P], ident[:, :]),
                          pe_tr if t == HALF - 1 else None)
            act.wait(m)
            return m, evac_split(bank, psum[:, bank, :], hi, lo, wait_free, *then)

        def mm_split(o, terms, done, start=True, stop=True):
            ops = [p for (lh, ll), (rh, rl) in terms for p in ((lh, rh), (lh, rl), (ll, rh))]
            for n, (l, r) in enumerate(ops):
                last = n == len(ops) - 1
                m = mm(o, l, r, start and n == 0, stop and last, done if last else None)
            return m

        def split_weight(where, name, src, shape, raw, sig):
            hi, lo = sb(where, name + "_hi", shape, f32r), sb(where, name + "_lo", shape, f32r)
            raw = raw.rearrange("p (c n) -> p c n", c=shape[1])
            m = sp.dma(raw, src, sig)
            act.wait(m)
            h = act.do(lambda e: e.activation(hi[:, :, :], raw, ACT.Copy), act_w)
            dve.wait(m, h)
            return (hi, lo), dve.do(lambda e: e.tensor_tensor(lo[:, :, :], raw, plain(hi[:, :, :]), ALU.subtract), dve_w)

        def rows(w):
            return w.rearrange("(c p) n -> p c n", p=P)

        TWO_PI = 2 * np.pi
        C1 = 6.28125
        C2 = float(np.float32(TWO_PI - C1))
        C3 = float(TWO_PI - C1 - C2)
        PI_BELOW = float(np.nextafter(np.float32(np.pi), np.float32(0)))
        ROUND = 1.5 * 2.0 ** 23

        def trig_units(areas):
            *angles, noise, turns = areas
            units = []
            for n, (w, w_noise) in enumerate(((theta, theta_n), (phi, phi_n))):
                ang = angles[n]
                quarter, shift = (0.25, float(np.pi / 2)) if n == 0 else (0.0, 0.0)

                def load(ang=ang, w=w, w_noise=w_noise):
                    sp.wait(free["spare"], free.get("noise"))
                    sp.dma(ang.rearrange("p (c d) -> p c d", c=KC), rows(w), ld[4])
                    a = sp.dma(noise.rearrange("p (c d) -> p c d", c=KC), rows(w_noise), ld[4])
                    dve.wait(a)
                steps = [lambda e, ang=ang: e.tensor_tensor(ang, ang, noise, ALU.add),
                         lambda e, ang=ang, quarter=quarter: e.tensor_scalar(turns, ang, 1 / TWO_PI, quarter,
                                                                             ALU.mult, ALU.add),
                         lambda e: e.tensor_scalar(turns, turns, ROUND, None, ALU.add),
                         lambda e: e.tensor_scalar(turns, turns, -ROUND, None, ALU.add)]
                steps += [lambda e, c=c, ang=ang: e.scalar_tensor_tensor(ang, turns, -c, ang, ALU.mult, ALU.add)
                          for c in (C1, C2, C3)]
                steps += [lambda e, ang=ang, shift=shift: e.tensor_scalar(ang, ang, shift, PI_BELOW, ALU.add, ALU.min),
                          lambda e, ang=ang: e.tensor_scalar(ang, ang, -PI_BELOW, None, ALU.max)]

                def run(ops):
                    for op in ops:
                        m = dve.do(op, dve_w)
                        dve.wait(m)
                    free["noise"] = m
                units += [load] + [lambda ops=steps[k:k + 3]: run(ops) for k in range(0, len(steps), 3)]

            def waves():
                act.wait(free["noise"])
                for n, ang in enumerate(angles):
                    m = act.do(lambda e, ang=ang: e.activation(ang, ang, ACT.Sin), act_w)
                act.wait(m)
                for n, ang in enumerate(angles):
                    hi, lo = (t[:, :, n * D:(n + 1) * D] for t in trig)
                    wave = ang.rearrange("p (c d) -> p c d", c=KC)
                    m = act.do(lambda e, hi=hi, wave=wave: e.activation(hi, wave, ACT.Copy), act_w)
                    dve.wait(m)
                    m = dve.do(lambda e, hi=hi, lo=lo, wave=wave: e.tensor_tensor(lo, wave, plain(hi), ALU.subtract), dve_w)
                free["areas"] = m
            return units + [waves]

        PIECE = 512
        pieces = [(name, w, c, o, min(PIECE, w.shape[1])) for name, w in
                  (("w1", w1T), ("w2", w2T), ("h1", h1T), ("h2", h2T), ("w3", w3T))
                  for c in range(w.shape[0] // P) for o in range(0, w.shape[1], PIECE)]
        changed = sb(early, "changed", [P, len(pieces)])
        counted = []

        def rounding(raw, hi, todo, late, free_from=None):
            bufs, loads, done = raw.shape[1], [], [0]

            def load(mark):
                if len(loads) < len(todo):
                    name, w, c, o, cols = pieces[todo[len(loads)]]
                    k = len(loads) % bufs
                    sp.wait(mark)
                    loads.append(sp.dma(raw[:, k, 0:cols], w[c * P:(c + 1) * P, o:o + cols], ld_c[k]))
            for _ in range(bufs):
                load(free_from)

            def unit():
                if done[0] == len(todo):
                    return False
                k, n = done[0] % bufs, todo[done[0]]
                loaded, cols = loads[done[0]], pieces[n][-1]
                done[0] += 1
                r, h = raw[:, k, 0:cols], hi[:, k, 0:cols]
                act.wait(loaded)
                a = act.do(lambda e: e.activation(h, r, ACT.Copy), act_c)

                def compare():
                    dve.wait(loaded, a)
                    d = dve.do(lambda e: e.scalar_tensor_tensor(r, r, 1.0, plain(h), ALU.mult, ALU.not_equal,
                                                                accum_out=changed[:, n:n + 1]), dve_c)
                    load(d)
                    counted[:] = [d]
                late.append(compare)
                return True
            return unit

        SC0 = 1.0 / D ** 0.5
        def layer1(ph):
            room_for(ph, 1, 0, 2)
            room["xn"], free["xn"] = shared_xn, [[]]
            xn, y = room["xn"], room["y"]
            flat_y = y[:, :, :, :].rearrange("p h t d -> p (h t d)")
            load_x(1)
            xT = [sb(ph, f"xT0_{k}", [P, KC, S], f32r) for k in ("hi", "lo")]
            qT = [[sb(ph, f"qT{i}_{k}", [P, KC, S], f32r) for k in ("hi", "lo")] for i in range(2)]
            kT = [[sb(ph, f"kT{i}_{k}", [P, KC, S], f32r) for k in ("hi", "lo")] for i in range(2)]
            v = [[sb(ph, f"v{i}_{k}", [P, ST, D], f32r) for k in ("hi", "lo")] for i in range(2)]
            raw = sb(ph, "raw", [P, 2, PIECE])
            raw_hi = sb(ph, "raw_hi", [P, 2, PIECE], f32r)
            prob = sb(ph, "prob", [P, 2, S])
            pT = [sb(ph, f"pT_{k}", [P, ST, P], f32r) for k in ("hi", "lo")]
            mx = sb(ph, "mx0", [P, 2])
            nb = sb(ph, "nb0", [P, 2])
            den = sb(ph, "den0", [P, 2])
            rden = sb(ph, "rden0", [P, 2])
            xT_free, qkv_free = [], [[], []]
            ring = [4]

            def next_bank():
                ring[0] = ring[0] + 1 if ring[0] < 7 else 4
                return ring[0]

            def pre_units(b, spare=None):
                def tr(half, c, done):
                    cols = slice(half * BANK, (half + 1) * BANK)
                    apart = half == 1 and spare is not None
                    m, mark = transpose_half(next_bank(), spare if apart else xn[:, 0, :, :], done["xn"], c, xT[0][:, c, cols],
                                             xT[1][:, c, cols], xT_free)
                    if apart:
                        free["spare"] = m
                    else:
                        free["xn"][0] = [m]
                    xT_ready[(b, half)] = mark

                def second(src, ready, done):
                    tiles = list(range(HALF))

                    def stats():
                        done["rstd"] = norm_stats("out", lambda t: src[:, t, :], ready, tiles)

                    def apply():
                        done["xn"] = norm_apply("out", done["rstd"], lambda t: src[:, t, :], lambda t: spare[:, t, :], tiles)
                    return [stats, apply]
                units = []
                for half in range(2):
                    t0 = b * ST + HALF * half
                    units_n, done = norm_in(b, half, x[:, t0:t0 + HALF, :], lambda t0=t0: x_ready[t0:t0 + HALF])
                    if half and spare is not None:
                        done = {}
                        units_n = second(x[:, t0:t0 + HALF, :], x_ready[t0:t0 + HALF], done)
                    units += units_n + [lambda c=c, half=half, done=done: tr(half, c, done) for c in range(KC)]
                return units

            def proj_units(b):
                def qk(dst, w, c, half):
                    bank = next_bank()
                    pe.wait(*bank_free[bank], xT_ready[(b, half)])
                    cols = slice(half * BANK, (half + 1) * BANK)
                    m = mm_split(psum[:, bank, :], [((w[0][:, k, c * P:(c + 1) * P], w[1][:, k, c * P:(c + 1) * P]),
                                                     (xT[0][:, k, cols], xT[1][:, k, cols])) for k in range(KC)], pe_prod)
                    act.wait(m)
                    qkv_ready[b] = evac_split(bank, psum[:, bank, :], dst[0][:, c, cols], dst[1][:, c, cols], qkv_free[b % 2])
                    return m

                def val(t):
                    bank = next_bank()
                    pe.wait(*bank_free[bank], xT_ready[(b, 1)])
                    w = wts[2]
                    for n in range(2):
                        tok = slice((t + n) * P, (t + n + 1) * P)
                        m = mm_split(psum[:, bank, n * D:(n + 1) * D], [((xT[0][:, k, tok], xT[1][:, k, tok]),
                                                                         (w[0][:, k, :], w[1][:, k, :])) for k in range(KC)],
                                     pe_prod)
                    act.wait(m)
                    qkv_ready[b] = evac_split(bank, psum[:, bank, :].rearrange("p (t d) -> p t d", t=2),
                                              v[b % 2][0][:, t:t + 2, :], v[b % 2][1][:, t:t + 2, :], qkv_free[b % 2])
                    xT_free[:] = [m]
                return ([lambda c=c, half=half, dst=dst, w=w: qk(dst, w, c, half)
                         for half in range(2) for dst, w in ((qT[b % 2], wts[0]), (kT[b % 2], wts[1])) for c in range(KC)]
                        + [lambda t=t: val(t) for t in range(0, ST, 2)])

            wts = []
            xT_ready, qkv_ready = {}, {}
            y_ready = {}
            st = {}

            def scores(b, i):
                n, Q, K = b * ST + i, qT[b % 2], kT[b % 2]
                k = n % 2
                pair = (2 * k, 2 * k + 1)
                pe.wait(*bank_free[pair[0]], qkv_ready[b])
                tok = slice(i * P, (i + 1) * P)
                w_all = (i + 1) * P
                for c0 in range(0, w_all, BANK):
                    w = min(BANK, w_all - c0)
                    mm_split(psum[:, pair[c0 // BANK], 0:w],
                             [((Q[0][:, kk, tok], Q[1][:, kk, tok]), (K[0][:, kk, c0:c0 + w], K[1][:, kk, c0:c0 + w]))
                              for kk in range(KC)], None, stop=c0 + w < w_all)
                d = i * P % BANK
                m = mm(psum[:, pair[i * P // BANK], d:d + P], ident16[:, :], tri16[:, :], False, True, pe_s)
                src = psum[:, pair[0]:pair[0] + 2, :].rearrange("p a n -> p (a n)")[:, 0:w_all]
                dve.wait(m, *st.get(("exp", n - 2), []))
                a = dve.do(lambda e: e.tensor_reduce(mx[:, k:k + 1], src, AX.X, ALU.max), dve_max)
                dve.wait(a)
                a = dve.do(lambda e: e.tensor_scalar(nb[:, k:k + 1], mx[:, k:k + 1], -SC0, None, ALU.mult), dve_max)
                st[("nb", n)] = a

            def exps(b, i):
                n = b * ST + i
                k = n % 2
                w_all = (i + 1) * P
                pair = (2 * k, 2 * k + 1)
                src = psum[:, pair[0]:pair[0] + 2, :].rearrange("p a n -> p (a n)")[:, 0:w_all]
                act.wait(st[("nb", n)], *st.get(("pT", n - 2), []), *st.get(("rden", n - 2), []))
                ex = act.do(lambda e: e.activation(prob[:, k, 0:w_all], src, ACT.Exp, bias=nb[:, k:k + 1], scale=SC0,
                                                   accum_out=den[:, k:k + 1]), act_exp)
                bank_free[pair[0]] = bank_free[pair[1]] = [ex]
                st[("exp", n)] = [ex]

            def turn(b, i):
                n = b * ST + i
                k = n % 2
                pe.wait(*st[("exp", n)])
                dve.wait(*st[("exp", n)])
                rd = dve.do(lambda e: e.reciprocal(rden[:, k:k + 1], den[:, k:k + 1]), dve_max)
                st[("rden", n)] = [rd]
                for k0 in range(0, i + 1, 4):
                    kk = min(4, i + 1 - k0)
                    bank = next_bank()
                    pe.wait(*bank_free[bank])
                    for j in range(kk):
                        m = pe.do(lambda e, j=j, bank=bank, k0=k0: e.transpose(psum[:, bank, j * P:(j + 1) * P],
                                                                  prob[:, k, (k0 + j) * P:(k0 + j + 1) * P], ident[:, :]),
                                  pe_tr)
                    act.wait(m)
                    st[("pTr", n)] = [evac_split(bank, psum[:, bank, 0:kk * P].rearrange("p (k q) -> p k q", q=P),
                                                 pT[0][:, k0:k0 + kk, :], pT[1][:, k0:k0 + kk, :],
                                                 st.get(("pv", n - 1), []))]
                st[("pT", n)] = [m]

            def weigh(b, i):
                n, V, O = b * ST + i, v[b % 2], next_bank()
                half, t = i // HALF, i % HALF
                pe.wait(*st[("pTr", n)], *bank_free[O])
                m = mm_split(psum[:, O, 0:D], [((pT[0][:, j, :], pT[1][:, j, :]), (V[0][:, j, :], V[1][:, j, :]))
                                               for j in range(i + 1)], pe_pv)
                st[("pv", n)] = [m]
                act.wait(m, *st[("rden", n)], *free["y"][half])
                o = act.do(lambda e: e.activation(y[:, half, t, :], psum[:, O, 0:D], ACT.Copy,
                                                  scale=rden[:, n % 2:n % 2 + 1]), act_out)
                st[("rden", n)] = [o]
                bank_free[O] = [o]
                if i == ST - 1:
                    qkv_free[b % 2] = [m]
                if t == HALF - 1:
                    t0 = b * ST + HALF * half

                    def then(m):
                        x_ready[t0:t0 + HALF] = [m] * HALF
                    stats, normalise = add_out(half, lambda: [o], x[:, t0:t0 + HALF, :], lambda: x_ready[t0:t0 + 1], then)
                    out_units.extend([stats, lambda: None, normalise])

            out_units, late = [], []
            start = pre_units(0, raw[:, :, :].rearrange("p k (t d) -> p (k t) d", d=D))
            for k in (0, 4):
                start[k]()
            for n, w in enumerate((wq0, wk0, wv0)):
                t, w_ready = split_weight(ph, f"w0{n}", rows(w), [P, KC, D], flat_y[:, n * KC * D:(n + 1) * KC * D], ld[n])
                wts.append(t)
            pe.wait(w_ready)
            for n in range(2, 2 * B):
                load_x(n)
            next_pre = pre_units(1)
            for u in (start[1], start[5], *start[2:4], next_pre[0], *start[6:], *proj_units(0), next_pre[1]):
                u()
            free["y"] = [[w_ready], [w_ready]]
            trig_side = trig_units([raw[:, 0, :], raw[:, 1, :], plain(raw_hi[:, 0, :]), plain(raw_hi[:, 1, :])])
            in_first = B * ST - len(trig_side)
            pre = {b: pre_units(b) if b > 1 else next_pre for b in range(1, B)}
            for b in range(B):
                side = [[] for _ in range(ST)]
                if b + 1 < B:
                    _, _, t00, t01, s1_, n1_, t10, t11 = pre[b + 1]
                    p_ = proj_units(b + 1)
                    side = [[t00, t01, s1_, p_[0]], [p_[1], n1_, p_[2]], [p_[3], t10, t11], [p_[4], p_[5]], [p_[6], p_[7]],
                            [p_[8], p_[9]], [p_[10]], [p_[11]]]
                if b == B - 1:
                    tail, _ = norm_in(0, 0, x[:, 0:HALF, :], x_ready[0:HALF])
                    side[4].append(tail[0])
                    side[6].append(tail[1])
                if b + 2 < B:
                    side[ST - 2].append(pre[b + 2][0])
                    side[ST - 1].append(pre[b + 2][1])
                for i in range(ST):
                    n = b * ST + i
                    scores(b, i)
                    if n >= 1:
                        turn(*divmod(n - 1, ST))
                    exps(b, i)
                    for u in side[i]:
                        u()
                    if n >= 1:
                        weigh(*divmod(n - 1, ST))
                    if out_units:
                        out_units.pop(0)()
                    if trig_side:
                        trig_side.pop(0)()
                        if not trig_side:
                            round_unit = rounding(raw, raw_hi, range(in_first), late, free["areas"])
                    else:
                        while late:
                            late.pop(0)()
                        round_unit()
            while late:
                late.pop(0)()
            turn(B - 1, ST - 1)
            weigh(B - 1, ST - 1)
            for u in out_units:
                u()
            barrier()
            return in_first

        with ExitStack() as ph:
            in_first = layer1(ph)

        def layer2(ph, in_first):
            room_for(ph, 2, 2, 2)
            room["roots"], room["apply"]["out"] = True, act
            xn, y = room["xn"], room["y"]
            xT = [[sb(ph, f"xT1_{i}{k}", [P, KC, BANK], f32r) for k in ("hi", "lo")] for i in range(2)]
            sq = sb(ph, "sq", [P, 2, 2 * D])
            pw = sb(ph, "pw", [P, 2, HALF, D])
            raw = sb(ph, "raw2", [P, 4, PIECE])
            raw_hi = sb(ph, "raw_hi2", [P, 4, PIECE], f32r)
            late = []
            round_unit = rounding(raw, raw_hi, range(in_first, len(pieces)), late)
            cnt = sb(ph, "cnt", [P, 1])
            xT_free = [[], []]
            sq_free, pw_free = [[], []], [[], []]
            ready, outs = {}, []
            ring = [0]

            def next_bank():
                ring[0] = (ring[0] + 1) % 8
                return ring[0]

            def pre_half(n):
                half, t0, k = n % 2, n * HALF, n % 2
                units, done = norm_in(n // 2, half, x[:, t0:t0 + HALF, :], x_ready[t0:t0 + HALF])
                source = xn[:, half, :, :]
                if n == 0:
                    units, done, source = [lambda: None] * 2, {"xn": None}, shared_xn[:, 0, :, :]

                def then(m):
                    ready[n] = m

                def tr(c):
                    m, _ = transpose_half(next_bank(), source, done["xn"], c, xT[k][0][:, c, :], xT[k][1][:, c, :],
                                          xT_free[k], then, late)
                    if n:
                        free["xn"][half] = [m]
                    else:
                        free["shared"] = m
                return units + [lambda: tr(0), lambda: tr(1)]

            def tile(n, t):
                k, q, bank = n % 2, t % 2, next_bank()
                pe.wait(*bank_free[bank], ready[n])
                tok = slice(t * P, (t + 1) * P)
                m = mm_split(psum[:, bank, :], [((xT[k][0][:, c, tok], xT[k][1][:, c, tok]),
                                                 (trig[0][:, c, :], trig[1][:, c, :])) for c in range(KC)], pe_prod)
                act.wait(m, *sq_free[q])
                s_ = act.do(lambda e: e.activation(sq[:, q, :], psum[:, bank, :], ACT.Square), act_h)
                bank_free[bank] = [s_]
                xT_free[k] = [m]

                def power():
                    dve.wait(s_, *pw_free[k])
                    d_ = dve.do(lambda e: e.tensor_tensor(pw[:, k, t, :], sq[:, q, 0:D], sq[:, q, D:2 * D], ALU.add), dve_h)
                    sq_free[q] = [d_]
                    if t == HALF - 1:
                        root(n, d_)
                late.append(power)

            def root(n, d_):
                half, k, t0 = n % 2, n % 2, n * HALF
                act.wait(d_, *free["y"][half])
                o = act.do(lambda e: e.activation(y[:, half, :, :], pw[:, k, :, :], ACT.Sqrt), act_out)
                pw_free[k] = [o]

                def then(m):
                    sp.wait(m)
                    xs_ready[(n // 2, half)] = sp.dma(half_of(xs, n // 2, half), x[:, t0:t0 + HALF, :], st_x)
                outs.extend(add_out(half, lambda: [o], x[:, t0:t0 + HALF, :], lambda: x_ready[t0:t0 + 1], then))

            pre = [pre_half(n) for n in range(2 * B)]
            tail = {}
            shared = shared_xn[:, 0, :, :]

            def tail_load():
                sp.wait(xs_ready[(0, 0)], free["shared"])
                tail["x"] = sp.dma(shared, half_of(xs, 0, 0), ld_a[0])

            def tail_stats():
                tail["rstd"] = norm_stats("in", lambda t: shared[:, t, :], [tail["x"]], list(range(HALF)))

            def tail_apply():
                norm_apply("in", tail["rstd"], lambda t: shared[:, t, :], lambda t: shared[:, t, :], list(range(HALF)))

            def finish_late():
                units, late[:] = list(late), []
                for u in units:
                    u()

            for u in pre[0] + pre[1][:2]:
                u()
                finish_late()
            for n in range(2 * B):
                for t in range(HALF):
                    tile(n, t)
                    if t in (1, 3) and n + 2 < 2 * B:
                        pre[n + 2][t // 2]()
                    if t in (0, 2) and outs:
                        outs.pop(0)()
                    finish_late()
                    if t < 2 and n + 1 < 2 * B:
                        pre[n + 1][t + 2]()
                    if n == 2 * B - 1 and t in (0, 1, 3):
                        (tail_load, tail_stats, None, tail_apply)[t]()
                    round_unit()
            finish_late()
            while outs:
                outs.pop(0)()
            while round_unit():
                finish_late()
            dve.wait(*counted)
            m = dve.do(lambda e: e.tensor_reduce(cnt[:, :], changed[:, :], AX.X, ALU.add), dve_c)
            pe.wait(m, *bank_free[0])
            m = pe.do(lambda e: e.matmul(psum[0:1, 0, 0:1], cnt[:, :], one[:, :], start=True, stop=True), pe_m)
            dve.wait(m)
            m = dve.do(lambda e: e.tensor_scalar(flag[:, :], psum[0:1, 0, 0:1], 0.0, None, ALU.is_gt), dve_c)
            bank_free[0] = [m]
            barrier()

        with ExitStack() as ph:
            layer2(ph, in_first)
        room["roots"], room["apply"]["out"] = False, dve
        early.close()

        G = 4
        SC1 = 1.0 / DK ** 0.5
        NST = 3
        STEPS = [(c, j) for c in range(S // BANK) for j in range(4 * (c + 1))]
        NS = len(STEPS)
        LEAD = NS + 5
        KR = 3 * DK
        def layer3(ph):
            attn = sb(ph, "attn", [P, ST, D])
            flat = attn[:, :, :].rearrange("p t d -> p (t d)")
            xT = [sb(ph, f"xT2_{k}", [P, KC, BANK], f32r) for k in ("hi", "lo")]
            nat = {"q": [sb(ph, f"q_{k}", [P, 2, S], f32r) for k in ("hi", "lo")],
                   "k": [sb(ph, f"k_{k}", [P, 2, S], f32r) for k in ("hi", "lo")]}
            VW = DK + 1
            VB = 2 * DK
            va = [sb(ph, f"va{i}", [P, ST, H * VW + VB - VW]) for i in range(2)]
            Qs = [sb(ph, f"Qs{i}", [P, 2, S], f32r) for i in range(NST)]
            Ks = [sb(ph, f"Ks{i}", [P, 2, 2, S], f32r) for i in range(NST)]
            stage = {k: sb(ph, f"stage_{k}", [P, 2, S]) for k in "qk"}
            pr = sb(ph, "pr", [P, 4, 2, BANK])
            maskw = sb(ph, "maskw", [P, BANK])
            mxs = sb(ph, "mxs", [P, 2, 2, 2, ST])
            mT = [sb(ph, f"mT_{k}", [2 * 2 * ST, P], f32r) for k in ("hi", "lo")]
            oT = sb(ph, "oT", [P, BANK])
            room_for(ph, 3, 0, 2, attn[:, :, :].rearrange("p (h t) d -> p h t d", h=2))
            room["xn"], free["xn"] = shared_xn, [[]]
            xn, y = room["xn"], room["y"]
            aT = [sb(ph, f"aT_{k}", [P, KC, 2 * P], f32r) for k in ("hi", "lo")]
            xr = sb(ph, "xr3", [P, HALF, D])
            rd4 = sb(ph, "rd4", [P, HALF * 4])

            m = pool.do(lambda e: e.memset(maskw[:, :], 0.0), pool_const)
            pool.wait(m)
            pool.do(lambda e: e.affine_select(out=maskw[:, BANK - P:], in_=maskw[:, BANK - P:], compare_op=ALU.is_ge,
                                              fill=NEG, base=0, pattern=[[-1, P]], channel_multiplier=1), pool_const)
            for t in (va[0], va[1]):
                pool.do(lambda e, t=t: e.memset(t[:, :, :], 1.0), pool_const)
            m = pool.do(lambda e: e.memset(stage["q"][:, :, :], 0.0), pool_const)
            later = [pool.do(lambda e: e.memset(Ks[2][:, :, :, :].bitcast(f32), 0.0), pool_const)]
            constants = [m, dve.do(lambda e: e.memset(stage["k"][:, :, :], 1.0), dve_w)]

            def init_done():
                for e in engines:
                    e.wait(*constants)

            def zero_keys(i):
                later.append(dve.do(lambda e: e.memset(Ks[i][:, :, :, :].bitcast(f32), 0.0), dve_w))

            MAXB, SIDE, STB, PVB = (0, 1, 6), 2, (3, 4, 5), 7
            xT_free, nat_free, va_free = [], [], [[], []]
            xT_ready, nat_ready, va_ready = {}, {}, {}
            stack_ready, stack_free = {}, {}
            m_ready, max_done = {}, {}
            st = {}
            side_banks = [2, 3, 4, 5, 6, 7]

            def side_bank():
                side_banks.append(side_banks.pop(0))
                return side_banks[-1]

            late = []

            def pre3(b, half, spare=None):
                way, buf = ("in", xn[:, 0, :, :]) if spare is None else ("out", spare)
                done = {"xn": None}

                def load():
                    sp.wait(xs_ready[(b, half)], *free["xn"][0])
                    done["x"] = sp.dma(buf, half_of(xs, b, half), ld_r if way == "out" else ld_a[0])

                def stats(tiles):
                    done["rstd"] = norm_stats(way, lambda t: buf[:, t, :], [done["x"]], tiles)

                def apply(tiles):
                    done["xn"] = norm_apply(way, done["rstd"], lambda t: buf[:, t, :], lambda t: buf[:, t, :], tiles)

                def tr(c):
                    def then(m):
                        xT_ready[(b, half)] = m
                    m, _ = transpose_half(side_bank(), buf, done["xn"], c, xT[0][:, c, :], xT[1][:, c, :], xT_free,
                                          then, late)
                    if way == "in":
                        free["xn"][0] = [m]
                    else:
                        st["xr_free"] = [m]
                return [load, *[lambda tiles=tiles, f=f: f(tiles) for f in (stats, apply) for tiles in tiles_of(2)],
                        lambda: tr(0), lambda: tr(1)]

            def proj3(b, half):
                def qk(name, c):
                    o = (0 if name == "q" else D) + c * P
                    cols = slice(half * BANK, (half + 1) * BANK)
                    bank = side_bank()
                    pe.wait(*bank_free[bank], xT_ready[(b, half)])
                    m = mm_split(psum[:, bank, :], [((wa_hi[:, k, o:o + P], wa_lo[:, k, o:o + P]),
                                                     (xT[0][:, k, :], xT[1][:, k, :])) for k in range(KC)], pe_prod)
                    act.wait(m)
                    hi, lo = nat[name]

                    def then(m):
                        nat_ready[b] = m
                    evac_split(bank, psum[:, bank, :], hi[:, c, cols], lo[:, c, cols], nat_free, then, late)

                def val(t):
                    bank = side_bank()
                    pe.wait(*bank_free[bank], xT_ready[(b, half)])
                    for n in range(2):
                        tok = slice((t + n) * P, (t + n + 1) * P)
                        m = mm_split(psum[:, bank, n * D:(n + 1) * D],
                                     [((xT[0][:, k, tok], xT[1][:, k, tok]), (wa_hi[:, k, 2 * D:], wa_lo[:, k, 2 * D:]))
                                      for k in range(KC)], pe_prod)
                    act.wait(m, *va_free[b % 2])
                    for n in range(2):
                        dst = va[b % 2][:, HALF * half + t + n, 0:H * VW].rearrange("p (h w) -> p h w", w=VW)[:, :, 0:DK]
                        o = act.do(lambda e, n=n, dst=dst: e.activation(
                            dst, psum[:, bank, n * D:(n + 1) * D].rearrange("p (h w) -> p h w", w=DK), ACT.Copy), act_out)
                    bank_free[bank] = [o]
                    va_ready[b] = o
                    xT_free[:] = [m]
                return ([lambda name=name, c=c: qk(name, c) for name in "qk" for c in range(2)]
                        + [lambda t=t: val(t) for t in range(0, HALF, 2)])

            def load_stack(g, issuers=(sp,), half=None):
                b, gl = divmod(g, G)
                cols = slice(0, S) if half is None else slice(half * BANK, (half + 1) * BANK)
                for e in issuers:
                    e.wait(nat_ready[b], *st.get("staged", []))
                marks = {}
                for side in range(2):
                    r = 32 * gl + DK * side
                    for k, (q_, k_) in enumerate(((0, 0), (1, 0), (0, 1))):
                        d = 64 * side + DK * k
                        for name, part in (("q", q_), ("k", k_)):
                            n = count["stack"] % len(issuers)
                            count["stack"] += 1
                            marks[n] = issuers[n].dma(stage[name][d:d + DK, :, cols], nat[name][part][r:r + DK, :, cols],
                                                      dma_stack[n])
                st[("stage", g)] = list(marks.values())
                if gl == G - 1:
                    nat_free[:] = st[("stage", g)]

            def copy_stack(g, k):
                i = g % NST
                if k < 2:
                    dst, src = Qs[i][:, k, :], stage["q"][:, k, :]
                else:
                    side, pair = divmod(k - 2, 2)
                    r = slice(64 * side, 64 * side + 64)
                    dst, src = Ks[i][r, side, pair, :], stage["k"][r, pair, :]
                marks = (*st[("stage", g)], *stack_free.get(g - NST, []))
                if k < 2 and g == 0:
                    dve.wait(*marks)
                    m = dve.do(lambda e: e.tensor_copy(dst, src), dve_w)
                elif k < 2:
                    pool.wait(*marks)
                    m = pool.do(lambda e: e.tensor_copy(dst, src), pool_stack)
                else:
                    act.wait(*marks)
                    m = act.do(lambda e: e.activation(dst, src, ACT.Copy), act_stack)
                stack_ready.setdefault(g, []).append(m)
                st["staged"] = stack_ready[g]

            max_blocks = [(i, k0, min(BANK, (i + 1) * P - k0)) for i, k0 in (
                (0, 0), (1, 0), (3, 0), (4, 0), (5, 0), (2, 0), (7, 0), (7, BANK), (6, 0), (6, BANK), (5, BANK), (4, BANK))]
            count = {"max": 0, "st": 0, "stack": 0}

            def max_unit(g, n, pair, side):
                i, k0, w = max_blocks[n]
                buf, mb = g % NST, g % 2
                diag = k0 + w == (i + 1) * P
                if n == 0:
                    dve.wait(*st.get(("mread", g - 2), []))
                bank = MAXB[count["max"] % len(MAXB)]
                count["max"] += 1
                pe.wait(*stack_ready[g], *bank_free[bank])
                m = mm(psum[:, bank, 0:w], Qs[buf][:, pair, i * P:(i + 1) * P], Ks[buf][:, side, pair, k0:k0 + w],
                       True, True, pe_max)
                dst = mxs[:, mb, side, pair, i:i + 1]
                dve.wait(m)
                if not diag:
                    a = dve.do(lambda e: e.tensor_reduce(dst, psum[:, bank, 0:w], AX.X, ALU.max), dve_max)
                    st[("part", side, pair, i)] = a
                else:
                    first = NEG
                    if k0:
                        dve.wait(st[("part", side, pair, i)])
                        first = dst
                    a = dve.do(lambda e: e.tensor_tensor_reduce(
                        out=psum[:, bank, 0:w], in0=psum[:, bank, 0:w], in1=maskw[:, BANK - w:], scale=1.0, scalar=first,
                        op0=ALU.add, op1=ALU.max, accum_out=dst), dve_max)
                bank_free[bank] = [a]
                st[("mx", g)] = a

            def put_max(g):
                mb = g % 2
                n = 2 * 2 * ST
                pe.wait(*bank_free[SIDE], st[("mx", g)])
                m = pe.do(lambda e: e.transpose(psum[0:n, SIDE, 0:P], mxs[:, mb, :, :, :].rearrange("p s a t -> p (s a t)"),
                                                ident[:, :]), pe_m)
                st[("mread", g)] = [m]
                act.wait(m, *st.get("m_sent", []))
                h = act.do(lambda e: e.activation(mT[0][:, :], psum[0:n, SIDE, 0:P], ACT.Copy, scale=-1.0), act_m)
                late.append(lambda: put_max_rest(g, h))

            def put_max_rest(g, h):
                buf, n = g % NST, 2 * 2 * ST
                dve.wait(h, *st.get("m_sent", []))
                l = dve.do(lambda e: e.scalar_tensor_tensor(mT[1][:, :], psum[0:n, SIDE, 0:P], -1.0, plain(mT[0][:, :]),
                                                            ALU.mult, ALU.subtract), dve_m)
                bank_free[SIDE] = [l]
                pool.wait(h, l)
                for side in range(2):
                    for k in range(2):
                        d = 64 * side + KR + k
                        a = pool.dma(Qs[buf][d:d + 1, :, :].rearrange("o a (t q) -> o (a t) q", q=P),
                                   mT[k][2 * ST * side:2 * ST * (side + 1), :], dma_m[buf])
                m_ready[g] = a
                st["m_sent"] = [a]

            def st_unit(s, pair, side):
                g, n = divmod(s, NS)
                c, j = STEPS[n]
                buf = g % NST
                q0 = max(c * BANK, j * P)
                w = (c + 1) * BANK - q0
                bank = STB[count["st"] % len(STB)]
                count["st"] += 1
                slot = 2 * (s % 2) + pair
                diag = j * P >= c * BANK
                pe.wait(m_ready[g], *bank_free[bank])
                m = mm(psum[:, bank, 0:w], Ks[buf][:, side, pair, j * P:(j + 1) * P], Qs[buf][:, pair, q0:q0 + w],
                       True, not diag, None if diag else pe_s)
                if diag:
                    m = mm(psum[:, bank, 0:P], tri16[:, :], ident16[:, :], False, True, pe_s)
                act.wait(m, *st.get(("pv", s - 2), []))
                e_ = act.do(lambda e: e.activation(pr[:, slot, side, 0:w], psum[:, bank, 0:w], ACT.Exp, scale=SC1), act_exp)
                bank_free[bank] = [e_]
                st[("pr", s)] = e_
                if n == NS - 1:
                    stack_free[g] = [m]

            def pv_step(s):
                g, n = divmod(s, NS)
                b, gl = divmod(g, G)
                c, j = STEPS[n]
                q0 = max(c * BANK, j * P)
                w = (c + 1) * BANK - q0
                if j == 0:
                    pe.wait(*bank_free[PVB], va_ready[b])
                pe.wait(st[("pr", s)])
                for pair in range(2):
                    for side in range(2):
                        head, ct = 8 * pair + 2 * gl + side, 2 * pair + side
                        m = mm(psum[32 * ct:32 * ct + VB, PVB, BANK - w:BANK], va[b % 2][:, j, head * VW:head * VW + VB],
                               pr[:, 2 * (s % 2) + pair, side, 0:w], j == 0, j == 4 * c + 3,
                               pe_pv if pair and side else None)
                st[("pv", s)] = [m]
                if j == 4 * c + 3:
                    if c == 1 and gl == G - 1:
                        va_free[b % 2] = [m]

                    def keep():
                        dve.wait(m, *st.get("oT", []))
                        bank_free[PVB] = [dve.do(lambda e: e.tensor_copy(oT[:, :], psum[:, PVB, :]), dve_out)]
                        st[("o", g, c)] = bank_free[PVB][0]
                    late.append(keep)

            def unturn(g, c):
                b, gl = divmod(g, G)
                pe.wait(*bank_free[SIDE], st[("o", g, c)])
                for t in range(HALF):
                    m = pe.do(lambda e, t=t: e.transpose(psum[:, SIDE, t * P:(t + 1) * P], oT[:, t * P:(t + 1) * P],
                                                         ident[:, :]), pe_tr)
                st["oT"] = [m]
                late.append(lambda: unturn_rest(g, c, m))

            def unturn_rest(g, c, m):
                b, gl = divmod(g, G)
                src = psum[:, SIDE, :].rearrange("p (t h w) -> p t h w", t=HALF, w=VB)
                dve.wait(m)
                r = dve.do(lambda e: e.reciprocal(rd4[:, :].rearrange("p (t h) -> p t h", t=HALF), src[:, :, :, DK]), dve_out)
                dve.wait(r, *st.get(("attn_free", c), []), *free["y"][c])
                o = dve.do(lambda e: e.tensor_tensor(
                    attn[:, HALF * c:HALF * (c + 1), 64 * gl:64 * (gl + 1)].rearrange("p t (h w) -> p t h w", w=DK),
                    src[:, :, :, 0:DK],
                    rd4[:, :].rearrange("p (t h) -> p t h", t=HALF).unsqueeze(3).to_broadcast([P, HALF, 4, DK]), ALU.mult), dve_out)
                bank_free[SIDE] = [o]
                st[("attn", b, c)] = o

            def post3(b):
                def load(half):
                    sp.wait(xs_ready[(b, half)], *st.get("xr_free", []))
                    st["xr"] = sp.dma(xr[:, :, :], half_of(xs, b, half), ld_r)

                def tr(half, t):
                    pe.wait(*bank_free[SIDE], st[("attn", b, half)])
                    for c in range(KC):
                        for n in range(2):
                            m = pe.do(lambda e, c=c, n=n: e.transpose(
                                psum[:, SIDE, (2 * c + n) * P:(2 * c + n + 1) * P],
                                attn[:, HALF * half + t + n, c * P:(c + 1) * P], ident[:, :]),
                                pe_tr if c == KC - 1 and n == 1 else None)
                    act.wait(m)

                    def then(m):
                        st["aT"] = m
                    evac_split(SIDE, psum[:, SIDE, :].rearrange("p (c t) -> p c t", c=KC), aT[0][:, :, :], aT[1][:, :, :],
                               st.get("aT_free", []), then, late)

                def wo(half, t):
                    pe.wait(*bank_free[SIDE], st["aT"])
                    for n in range(2):
                        tok = slice(n * P, (n + 1) * P)
                        m = mm_split(psum[:, SIDE, n * D:(n + 1) * D], [((aT[0][:, k, tok], aT[1][:, k, tok]),
                                                                         (wo_hi[:, k, :], wo_lo[:, k, :])) for k in range(KC)],
                                     pe_prod)
                    act.wait(m)
                    o = act.do(lambda e: e.activation(y[:, half, t:t + 2, :],
                                                      psum[:, SIDE, :].rearrange("p (t d) -> p t d", t=2), ACT.Copy), act_out)
                    bank_free[SIDE] = [o]
                    st["aT_free"] = [m]
                    st[("y", half)] = o

                def then(half, m):
                    sp.wait(m)
                    xs_ready[(b, half)] = sp.dma(half_of(xs, b, half), xr[:, :, :], st_x)
                    st["xr_free"] = [xs_ready[(b, half)]]
                units = []
                for half in range(2):
                    units += [lambda half=half: load(half), lambda half=half: tr(half, 0), lambda half=half: wo(half, 0),
                              lambda half=half: tr(half, 2), lambda half=half: wo(half, 2),
                              *add_out(half, lambda half=half: [st[("y", half)]], xr[:, :, :], lambda: [st["xr"]],
                                       lambda m, half=half: then(half, m), 2)]
                return units

            def copy_units(g):
                return [lambda k=k: copy_stack(g, k) for k in range(6)]

            def run(units):
                for u in units:
                    u()
                    while late:
                        late.pop(0)()

            first, second = pre3(0, 0), pre3(0, 1, xr[:, :, :])
            (wa_hi, wa_lo), m1 = split_weight(ph, "wqkv", rows(wqkvT), [P, KC, 3 * D], flat[:, 0:KC * 3 * D], ld[0])
            (wo_hi, wo_lo), m2 = split_weight(ph, "wo", rows(woT), [P, KC, D], flat[:, KC * 3 * D:], ld[1])
            run(second[:3] + first[5:])
            pe.wait(m1, m2)
            half0, half1 = proj3(0, 0), proj3(0, 1)
            run(second[3:5] + half0[:4] + [init_done, lambda: load_stack(0, (sp, act), 0), lambda: zero_keys(0)])
            run(half0[4:] + second[5:] + half1[:4] + [lambda: load_stack(0, (sp, act, pool), 1), lambda: zero_keys(1)] + half1[4:])
            for e in engines:
                e.wait(*later)
            run(copy_units(0))
            side_banks[:] = [SIDE]
            total = B * G * NS
            plan = {}

            def at(steps, units):
                for step, unit in zip(steps, units, strict=True):
                    plan.setdefault(step, []).append(unit)

            for g in range(B * G):
                s0 = g * NS
                if g:
                    at([s0 - (27 if g % G else 23)], [lambda g=g: load_stack(g)])
                    at([s0 - n for n in ((24, 24, 23, 22, 20, 19) if g % G else (20, 20, 20, 19, 19, 18))], copy_units(g))
                at([s0 - 5], [lambda g=g: put_max(g)])
                at([s0 + 5, s0 + NS + 1], [lambda g=g: unturn(g, 0), lambda g=g: unturn(g, 1)])
            for b in range(B):
                s0, end = b * G * NS, (b + 1) * G * NS
                at([end + n for n in (-6, -6, -4, -3, -2, -1, 0, 3, 4, 5, 2, 3, 4, 6, 7, 8, 11, 12)], post3(b))
                if b + 1 < B:
                    at([s0 + n for n in (-14, -12, -11, -8, -7, -1, 0)], pre3(b + 1, 0))
                    at([s0 + n for n in (10, 11, 12, 14, 15, 16)], proj3(b + 1, 0))
                    at([s0 + n for n in (1, 9, 10, 13, 14, 18, 20)], pre3(b + 1, 1))
                    at([s0 + n for n in (21, 22, 23, 24, 26, 27)], proj3(b + 1, 1))
            start4 = total - 8

            first4 = shared_xn[:, 0, :, :]

            def load_first():
                sp.wait(xs_ready[(0, 0)], *free["xn"][0])
                st["first"] = sp.dma(first4[:, :, :], half_of(xs, 0, 0), ld_a[1])

            def first_stats():
                st["first_rstd"] = norm_stats("in", lambda t: first4[:, t, :], [st["first"]], list(range(HALF)))

            at([start4, start4 + 3, start4 + 5],
               [load_first, first_stats,
                lambda: norm_apply("in", st["first_rstd"], lambda t: first4[:, t, :], lambda t: first4[:, t, :], list(range(HALF)))])
            for s in range(-LEAD, total + 16):
                heads = [(pair, side) for pair in range(2) for side in range(2)]
                units = []
                for pair, side in heads:
                    if s + LEAD < total:
                        units.append(lambda pair=pair, side=side: max_unit(*divmod(s + LEAD, NS), pair, side))
                    if 0 <= s < total:
                        units.append(lambda pair=pair, side=side: st_unit(s, pair, side))
                if 0 <= s - 1 < total:
                    units.append(lambda: pv_step(s - 1))
                finish, late[:] = list(late), []
                for u in units[:4] + finish + units[4:] + plan.get(s, []):
                    u()
            barrier()

        with ExitStack() as ph:
            layer3(ph)

        def layer4(ph, fast):
            parts = ("hi", "lo") if fast else ("all",)
            dt = f32r if fast else f32
            tag = "f" if fast else "g"
            src = {"w1": w1T, "w2": w2T, "h1": h1T, "h2": h2T, "w3": w3T}
            loader = pool if fast else sp
            W, w_ready = {}, {}
            room_for(ph, 4 if fast else 5, 1, 1)
            xn, y = room["xn"], room["y"]
            NXA = 3
            xa = sb(ph, "xa" + tag, [P, NXA, HALF, D])
            xa_ready, xa_free = {}, [[] for _ in range(NXA)]

            def load_x(n):
                k = n % NXA
                sp.wait(xs_ready[divmod(n, 2)], *xa_free[k])
                xa_ready[n] = sp.dma(xa[:, k, :, :], half_of(xs, *divmod(n, 2)), ld_a[k])

            load_x(0)
            sc = {}
            for name, vec in (("s1", s1), ("s2", s2), ("h1", sh1), ("h2", sh2)):
                sc[name] = sb(ph, tag + "sc" + name, [P, HC])
                sp.dma(sc[name][:, :], vec, ld[5])
            s3b = sb(ph, tag + "s3b", [P, D])
            sc_ready = sp.dma(s3b[:, :], s3.to_broadcast([P, D]), ld[5])
            for name in src:
                W[name] = sb(ph, tag + "W" + name, [P, src[name].shape[0] // P, src[name].shape[1]], dt)

            def load_weights(names):
                for name in names:
                    n = 5 * (not fast) + list(src).index(name)
                    w_ready[name] = loader.dma(W[name][:, :, :], rows(src[name]), ld_w[n])
            act.wait(sc_ready)
            dve.wait(sc_ready)
            xT = {k: sb(ph, f"{tag}xT_{k}", [P, 2, KC, BANK], dt) for k in parts}
            hid = [{k: sb(ph, f"{tag}h{i}_{k}", [P, HC, BANK], dt) for k in parts} for i in range(2)]
            sil = sb(ph, tag + "sil", [P, 2, BANK])
            act_raw_buf = sb(ph, tag + "raw", [P, 2, BANK])
            xT_free, h_free, sil_free, raw_free = [[], []], [[], []], [[], []], [[], []]
            xT_ready, h_ready = {}, [{}, {}]
            bank_n, raw_n = [0], [0]

            def next_bank():
                bank_n[0] = (bank_n[0] + 1) % 8
                return bank_n[0]

            def views(buf, *at):
                return [buf[k][at] for k in parts]

            def products(outs, name, chunks, operands, ready):
                pe.wait(w_ready[name])
                marks = []
                for c in range(chunks):
                    pe.wait(ready(c))
                    for o, bank, which in outs:
                        if c == 0:
                            pe.wait(*bank_free[bank])
                        pairs = operands(which, c)
                        for n, (l, r) in enumerate(pairs):
                            last = c == chunks - 1 and n == len(pairs) - 1
                            m = mm(o, l, r, c == 0 and n == 0, last, pe_h if last else None)
                        if last:
                            marks.append(m)
                return marks

            def pre4(n):
                k = n % 2
                units, done = norm_in(n // 2, n % 2, xa[:, n % NXA, :, :], lambda: [xa_ready[n]])
                source = xn[:, 0, :, :]
                if n == 0:
                    units, done, source = [], {"xn": None}, shared_xn[:, 0, :, :]

                def tr(c):
                    bank = next_bank()
                    if fast:
                        m, mark = transpose_half(bank, source, done["xn"], c, xT["hi"][:, k, c, :],
                                                 xT["lo"][:, k, c, :], xT_free[k])
                    else:
                        pe.wait(*bank_free[bank], done["xn"])
                        for t in range(HALF):
                            m = pe.do(lambda e, t=t: e.transpose(psum[:, bank, t * P:(t + 1) * P],
                                                                 source[:, t, c * P:(c + 1) * P], ident[:, :]), pe_tr)
                        act.wait(m, *xT_free[k])
                        mark = act.do(lambda e: e.activation(xT["all"][:, k, c, :], psum[:, bank, :], ACT.Copy), act_hi)
                        bank_free[bank] = [mark]
                    free["xn"][0] = [m]
                    xT_ready[(n, c)] = mark
                return units + [lambda: tr(0), lambda: tr(1)]

            def keep(i, oc, raw, mark):
                if not fast:
                    return
                hi, lo = hid[i]["hi"][:, oc, :], hid[i]["lo"][:, oc, :]
                act.wait(mark, *h_free[i])
                h = act.do(lambda e: e.activation(hi, raw, ACT.Copy), act_hi)
                dve.wait(mark, h, *h_free[i])
                h_ready[i][oc] = dve.do(lambda e: e.tensor_tensor(lo, raw, plain(hi), ALU.subtract), dve_lo)

            def target(i, oc):
                if not fast:
                    return hid[i]["all"][:, oc, :], h_free[i], None
                k = raw_n[0] % 2
                raw_n[0] += 1
                return act_raw_buf[:, k, :], raw_free[k], k

            def gated(n, oc):
                k, q = n % 2, oc % 2
                ba, bb = next_bank(), next_bank()
                cols = slice(oc * P, (oc + 1) * P)

                def product(name, bank):
                    return products([(psum[:, bank, :], bank, None)], name, KC,
                                    lambda _, c: [(W[name][:, c, cols], x_) for x_ in views(xT, slice(None), k, c, slice(None))],
                                    lambda c: xT_ready[(n, c)])[0]
                ma = product("w1", ba)
                act.wait(ma, *sil_free[q])
                a_ = act.do(lambda e: e.activation(sil[:, q, :], psum[:, ba, :], ACT.Silu, scale=sc["s1"][:, oc:oc + 1]), act_h)
                bank_free[ba] = [a_]
                mb = product("w2", bb)
                dst, dst_free, r_ = target(k, oc)
                dve.wait(mb, a_, *dst_free)
                d_ = dve.do(lambda e: e.scalar_tensor_tensor(dst, psum[:, bb, :], sc["s2"][:, oc:oc + 1], sil[:, q, :],
                                                             ALU.mult, ALU.mult), dve_h)
                bank_free[bb], sil_free[q] = [d_], [d_]
                h_ready[k][oc] = d_
                keep(k, oc, dst, d_)
                if fast:
                    raw_free[r_] = [h_ready[k][oc]]
                xT_free[k] = [mb]

            def dense(i, name, ocs):
                banks = [next_bank() for _ in ocs]
                marks = products([(psum[:, bk, :], bk, oc) for bk, oc in zip(banks, ocs)], name, HC,
                                 lambda oc, c: [(W[name][:, c, oc * P:(oc + 1) * P], h)
                                                for h in views(hid[i], slice(None), c, slice(None))],
                                 lambda c: h_ready[i][c])
                for bk, oc, m in zip(banks, ocs, marks):
                    activate(i, name, oc, bk, m)
                h_free[i] = [m]

            def activate(i, name, oc, bk, m):
                dst, dst_free, r_ = target(1 - i, oc)
                act.wait(m, *dst_free)
                a_ = act.do(lambda e: e.activation(dst, psum[:, bk, :], ACT.Gelu, scale=sc[name][:, oc:oc + 1]), act_raw)
                bank_free[bk] = [a_]
                h_ready[1 - i][oc] = a_
                keep(1 - i, oc, dst, a_)
                if fast:
                    raw_free[r_] = [h_ready[1 - i][oc]]

            def last_product(n, t):
                i, bk = n % 2, next_bank()
                m = products([(psum[:, bk, 0:D], bk, None)], "w3", HC,
                             lambda _, c: [(h, W["w3"][:, c, :]) for h in views(hid[i], slice(None), c, slice(t * P, (t + 1) * P))],
                             lambda c: h_ready[i][c])[0]
                dve.wait(m, *free["y"][0])
                o = dve.do(lambda e: e.tensor_tensor(y[:, 0, t, :], psum[:, bk, 0:D], s3b[:, :], ALU.mult), dve_out)
                bank_free[bk] = [o]
                h_free[i] = [m]
                return o

            def finish(n, o):
                b, half = divmod(n, 2)
                k = n % NXA

                def then(m):
                    sp.wait(m)
                    xa_free[k] = [sp.dma(half_of(out, b, half), xa[:, k, :, :], st_out[k])]
                return add_out(half, lambda: [o], xa[:, k, :, :], lambda: [], then)

            load_weights(src)
            for u in pre4(0):
                u()
            outs, GRP = [], 4
            for oc in range(GRP):
                gated(0, oc)
            for n in range(2 * B):
                more = n + 1 < 2 * B
                if more:
                    load_x(n + 1)
                if n:
                    for t in range(HALF):
                        o = last_product(n - 1, t)
                    outs = finish(n - 1, o)
                for oc in range(GRP, HC):
                    gated(n, oc)
                side = (pre4(n + 1) if more else [lambda: None] * 4)
                side = [side[:1], side[1:2] + outs[:1], side[2:] + outs[1:], []]
                for i, name in ((n % 2, "h1"), (1 - n % 2, "h2")):
                    for oc in range(0, HC, GRP):
                        dense(i, name, range(oc, oc + GRP))
                        for u in side.pop(0):
                            u()
                if more:
                    for oc in range(GRP):
                        gated(n + 1, oc)
            for t in range(HALF):
                o = last_product(2 * B - 1, t)
            for u in finish(2 * B - 1, o):
                u()
            for marks in xa_free:
                sp.wait(*marks)

        for e in engines:
            e.before, e.queue = e.queue, []
        values, waited = [s.value for s in signals], [dict(e.waited) for e in engines]
        forms = []
        for fast in (False, True):
            for s, v in zip(signals, values):
                s.value = v
            for e, w in zip(engines, waited):
                e.waited, e.queue = dict(w), []
            free["in"], free["out"] = [], []
            for marks in bank_free:
                marks.clear()
            with ExitStack() as ph:
                layer4(ph, fast)
            forms.append([e.queue for e in engines])
        for e, general, quick in zip(engines, *forms):
            e.queue = e.before
            e.branch(flag[0:1, 0:1], general, quick)

        block = ctx.enter_context(nc.Block())
        block.tensor(lambda e: pe.emit(e))
        block.scalar(lambda e: act.emit(e))
        block.vector(lambda e: dve.emit(e))
        block.gpsimd(lambda e: pool.emit(e))
        block.sync(lambda e: sp.emit(e))


def kernel(**inputs):
    import concourse.bacc as bacc
    from concourse.bass_utils import run_bass_kernel_spmd as run

    a = {k: np.asarray(v) for k, v in inputs.items()}
    wo = a["L1_attn_w_o"].T.reshape(2, 4, 2, DK, D).transpose(1, 0, 2, 3, 4).reshape(D, D)
    laid = {
        "x": a["L0_attn_x"], "wq0": a["L0_attn_Wq"], "wk0": a["L0_attn_Wk"], "wv0": a["L0_attn_Wv"],
        "theta": a["L0_ffn_theta"], "phi": a["L0_ffn_phi"], "theta_n": a["L0_ffn_theta_noise"],
        "phi_n": a["L0_ffn_phi_noise"], "wqkvT": a["L1_attn_w_qkv"].reshape(3 * D, D).T, "woT": wo,
        "w1T": a["L1_ffn_w1_w"].T, "w2T": a["L1_ffn_w2_w"].T, "h1T": a["L1_ffn_h1_w"].T, "h2T": a["L1_ffn_h2_w"].T,
        "w3T": a["L1_ffn_w3_w"].T,
        "s1": a["L1_ffn_w1_s"].reshape(HC, P).T, "s2": a["L1_ffn_w2_s"].reshape(HC, P).T,
        "sh1": a["L1_ffn_h1_s"].reshape(HC, P).T, "sh2": a["L1_ffn_h2_s"].reshape(HC, P).T,
        "s3": a["L1_ffn_w3_s"].reshape(1, D),
    }
    nc = bacc.Bacc("TRN2", target_bir_lowering=False, num_devices=1)
    arrays, args = {}, []
    for name, v in laid.items():
        v = np.ascontiguousarray(v)
        arrays[f"in_{name}"] = v
        args.append(nc.dram_tensor(f"in_{name}", v.shape, mybir.dt.from_np(v.dtype), kind="ExternalInput").ap())
    args.append(nc.dram_tensor("out_x", (B, S, D), f32, kind="ExternalOutput").ap())
    sandwich(nc, *args)
    r = run(nc, [arrays], core_ids=[0])
    return r.results[0]["out_x"]
```
